# Optimizing a Trainium2 kernel written in Bass

```python
import numpy as np
import jax
import jax.numpy as jnp

def _softmax(x, axis=-1):
    return jax.nn.softmax(x, axis=axis)

def _gelu(x):
    return jax.nn.gelu(x, approximate=True)

def _silu(x):
    return jax.nn.silu(x)

def _sigmoid(x):
    return jax.nn.sigmoid(x)

def _layernorm(x, axis=-1, eps=1e-05):
    m = jnp.mean(x, axis=axis, keepdims=True)
    v = jnp.var(x, axis=axis, keepdims=True)
    return (x - m) / jnp.sqrt(v + eps)

def _scatter_add(tgt, idx, src, axis=0):
    return tgt.at[idx].add(src)

def _segment_sum(src, seg, n):
    return jax.ops.segment_sum(src, seg, n)
kernel_name = 'mk_hybrid_d1_jaxref_r8_48d409'

def setup_inputs(seed: int=0):
    np.random.seed(seed)
    _w = jnp.asarray

    def _L0_attn_a_setup():
        import jax, jax.numpy as jnp
        import numpy as np
        GAMMA = 0.9
        SCALE_BASE = 512.0

        def _xpos(x, downscale=False):
            B, L, D = x.shape
            half = D // 2
            scale_vec = (jnp.arange(0, D, 2, dtype=jnp.float32) + 0.4 * D) / (1.4 * D)
            power = jnp.arange(L, dtype=jnp.float32) / SCALE_BASE
            scale = scale_vec[None, :] ** power[:, None]
            if downscale:
                scale = 1.0 / scale
            inv_freq = 1.0 / 10000.0 ** (jnp.arange(half, dtype=jnp.float32) / half)
            sinusoid = jnp.arange(L, dtype=jnp.float32)[:, None] * inv_freq[None, :]
            sin = jnp.repeat(jnp.sin(sinusoid) * scale, 2, axis=-1)
            cos = jnp.repeat(jnp.cos(sinusoid) * scale, 2, axis=-1)
            x_even = x[..., 0::2]
            x_odd = x[..., 1::2]
            rot = jnp.stack((-x_odd, x_even), axis=-1).reshape(x.shape)
            return x * cos + rot * sin

        def _get_D(seq_len):
            n = jnp.arange(seq_len, dtype=jnp.float32)[:, None]
            m = jnp.arange(seq_len, dtype=jnp.float32)[None, :]
            D = GAMMA ** jnp.abs(n - m)
            return D
        key = jax.random.key(seed)
        k1, k2, k3, k4 = jax.random.split(key, 4)
        B, L, H, Dh = (8, 256, 128, 128)
        X = jax.random.normal(k1, (B, L, H), dtype=jnp.float32)
        W_Q = jax.random.normal(k2, (H, Dh), dtype=jnp.float32) / H
        W_K = jax.random.normal(k3, (H, Dh), dtype=jnp.float32) / H
        W_V = jax.random.normal(k4, (H, Dh), dtype=jnp.float32) / H
        return {'X': X, 'W_Q': W_Q, 'W_K': W_K, 'W_V': W_V}
    _L0_attn_a_in = _L0_attn_a_setup()

    def _L0_attn_b_setup():
        import jax, jax.numpy as jnp
        import numpy as np
        DIM = 128
        STATE = 32
        B, S = (4, 512)
        key = jax.random.key(seed)
        ks = jax.random.split(key, 8)
        sc_b = 1.0 / np.sqrt(DIM)
        sc_c = 1.0 / np.sqrt(STATE)
        return {'x': jax.random.normal(ks[0], (B, S, DIM), dtype=jnp.float32), 'A': jax.random.normal(ks[1], (STATE,), dtype=jnp.float32) * 0.02, 'B_w': jax.random.uniform(ks[2], (STATE, DIM), minval=-sc_b, maxval=sc_b), 'B_b': jax.random.uniform(ks[3], (STATE,), minval=-sc_b, maxval=sc_b), 'C_w': jax.random.uniform(ks[4], (DIM, STATE), minval=-sc_c, maxval=sc_c), 'C_b': jax.random.uniform(ks[5], (DIM,), minval=-sc_c, maxval=sc_c), 'D_w': jax.random.uniform(ks[6], (DIM, DIM), minval=-sc_b, maxval=sc_b), 'D_b': jax.random.uniform(ks[7], (DIM,), minval=-sc_b, maxval=sc_b)}
    _L0_attn_b_in = _L0_attn_b_setup()

    def _L0_ffn_setup():
        import jax, jax.numpy as jnp
        import numpy as np
        B, S, D = (4, 64, 128)
        E, K, H = (64, 8, 32)
        ES, HS = (2, 256)
        key = jax.random.key(seed)
        ks = jax.random.split(key, 8)
        scale = 0.02
        rn = lambda k, shape, s: jax.random.normal(k, shape, jnp.float32) * s
        return {'x': rn(ks[0], (B, S, D), 1.0), 'router_w': rn(ks[1], (D, E), scale), 'router_b': jnp.zeros((E,), jnp.float32), 'w1': rn(ks[2], (E, D, H), scale), 'b1': jnp.zeros((E, H), jnp.float32), 'w2': rn(ks[3], (E, H, D), scale), 'b2': jnp.zeros((E, D), jnp.float32), 'sw1': rn(ks[4], (ES, D, HS), scale), 'sb1': jnp.zeros((ES, HS), jnp.float32), 'sw2': rn(ks[5], (ES, HS, D), scale), 'sb2': jnp.zeros((ES, D), jnp.float32)}
    _L0_ffn_in = _L0_ffn_setup()
    _d = {'L0_attn_a_X': _L0_attn_a_in['X'], 'L0_attn_a_W_Q': _L0_attn_a_in['W_Q'], 'L0_attn_a_W_K': _L0_attn_a_in['W_K'], 'L0_attn_a_W_V': _L0_attn_a_in['W_V'], 'L0_attn_b_A': _L0_attn_b_in['A'], 'L0_attn_b_B_w': _L0_attn_b_in['B_w'], 'L0_attn_b_B_b': _L0_attn_b_in['B_b'], 'L0_attn_b_C_w': _L0_attn_b_in['C_w'], 'L0_attn_b_C_b': _L0_attn_b_in['C_b'], 'L0_attn_b_D_w': _L0_attn_b_in['D_w'], 'L0_attn_b_D_b': _L0_attn_b_in['D_b'], 'L0_ffn_router_w': _L0_ffn_in['router_w'], 'L0_ffn_router_b': _L0_ffn_in['router_b'], 'L0_ffn_w1': _L0_ffn_in['w1'], 'L0_ffn_b1': _L0_ffn_in['b1'], 'L0_ffn_w2': _L0_ffn_in['w2'], 'L0_ffn_b2': _L0_ffn_in['b2'], 'L0_ffn_sw1': _L0_ffn_in['sw1'], 'L0_ffn_sb1': _L0_ffn_in['sb1'], 'L0_ffn_sw2': _L0_ffn_in['sw2'], 'L0_ffn_sb2': _L0_ffn_in['sb2']}
    _x0 = _d['L0_attn_a_X']
    _d['L0_attn_a_X'] = jax.random.normal(jax.random.fold_in(jax.random.key(seed), 1), (8, 512, 128), dtype=_x0.dtype)
    del _x0
    return _d

def reference(L0_attn_a_X, L0_attn_a_W_Q, L0_attn_a_W_K, L0_attn_a_W_V, L0_attn_b_A, L0_attn_b_B_w, L0_attn_b_B_b, L0_attn_b_C_w, L0_attn_b_C_b, L0_attn_b_D_w, L0_attn_b_D_b, L0_ffn_router_w, L0_ffn_router_b, L0_ffn_w1, L0_ffn_b1, L0_ffn_w2, L0_ffn_b2, L0_ffn_sw1, L0_ffn_sb1, L0_ffn_sw2, L0_ffn_sb2):

    def _L0_attn_a_ref(X, W_Q, W_K, W_V):
        import jax, jax.numpy as jnp
        import numpy as np
        GAMMA = 0.9
        SCALE_BASE = 512.0

        def _xpos(x, downscale=False):
            B, L, D = x.shape
            half = D // 2
            scale_vec = (jnp.arange(0, D, 2, dtype=jnp.float32) + 0.4 * D) / (1.4 * D)
            power = jnp.arange(L, dtype=jnp.float32) / SCALE_BASE
            scale = scale_vec[None, :] ** power[:, None]
            if downscale:
                scale = 1.0 / scale
            inv_freq = 1.0 / 10000.0 ** (jnp.arange(half, dtype=jnp.float32) / half)
            sinusoid = jnp.arange(L, dtype=jnp.float32)[:, None] * inv_freq[None, :]
            sin = jnp.repeat(jnp.sin(sinusoid) * scale, 2, axis=-1)
            cos = jnp.repeat(jnp.cos(sinusoid) * scale, 2, axis=-1)
            x_even = x[..., 0::2]
            x_odd = x[..., 1::2]
            rot = jnp.stack((-x_odd, x_even), axis=-1).reshape(x.shape)
            return x * cos + rot * sin

        def _get_D(seq_len):
            n = jnp.arange(seq_len, dtype=jnp.float32)[:, None]
            m = jnp.arange(seq_len, dtype=jnp.float32)[None, :]
            D = GAMMA ** jnp.abs(n - m)
            return D
        B, L, H = X.shape
        D = _get_D(L)
        Q = _xpos(X @ W_Q)
        K = _xpos(X @ W_K, downscale=True)
        V = X @ W_V
        scores = jnp.einsum('bqd,bkd->bqk', Q, K)
        p_attn = jax.nn.softmax(scores, axis=-1)
        p_attn = p_attn * D[None, :, :]
        return jnp.einsum('bqk,bkv->bqv', p_attn, V)

    def _L0_attn_b_ref(x, A, B_w, B_b, C_w, C_b, D_w, D_b):
        import jax, jax.numpy as jnp
        import numpy as np
        DIM = 128
        STATE = 32
        B, S = (4, 512)
        Bu = jnp.einsum('bsd,nd->bsn', x, B_w) + B_b
        Du = jnp.einsum('bsd,ed->bse', x, D_w) + D_b
        Aexp = jnp.exp(A)[None, :]
        state0 = jnp.zeros((x.shape[0], A.shape[0]), dtype=x.dtype)

        def step(state, bu_t):
            state = jnp.tanh(state * Aexp + bu_t)
            return (state, state)
        _, states = jax.lax.scan(step, state0, jnp.swapaxes(Bu, 0, 1))
        states = jnp.swapaxes(states, 0, 1)
        y = jnp.einsum('bsn,en->bse', states, C_w) + C_b + Du
        return y

    def _L0_ffn_ref(x, router_w, router_b, w1, b1, w2, b2, sw1, sb1, sw2, sb2):
        import jax, jax.numpy as jnp
        import numpy as np
        B, S, D = (4, 64, 128)
        E, K, H = (64, 8, 32)
        ES, HS = (2, 256)
        b_, s_, d_ = x.shape
        xf = x.reshape(-1, d_)
        probs = jax.nn.softmax(xf @ router_w + router_b, axis=-1)
        tw, ti = jax.lax.top_k(probs, K)
        tw = tw / jnp.sum(tw, axis=-1, keepdims=True)

        def body(acc, p):
            W1, B1, W2, B2, e = p
            h = jax.nn.silu(xf @ W1 + B1) @ W2 + B2
            cw = jnp.sum(jnp.where(ti == e, tw, 0.0), axis=-1)
            return (acc + cw[:, None] * h, None)
        routed, _ = jax.lax.scan(body, jnp.zeros_like(xf), (w1, b1, w2, b2, jnp.arange(w1.shape[0])))

        def shared_mlp(W1, B1, W2, B2):
            return jax.nn.silu(xf @ W1 + B1) @ W2 + B2
        shared = jnp.sum(jax.vmap(shared_mlp)(sw1, sb1, sw2, sb2), axis=0)
        return (routed + shared).reshape(b_, s_, d_)
    x = L0_attn_a_X
    x = x + _L0_attn_a_ref(_layernorm(x, axis=-1), L0_attn_a_W_Q, L0_attn_a_W_K, L0_attn_a_W_V)
    x = x + _L0_ffn_ref(_layernorm(x, axis=-1), L0_ffn_router_w, L0_ffn_router_b, L0_ffn_w1, L0_ffn_b1, L0_ffn_w2, L0_ffn_b2, L0_ffn_sw1, L0_ffn_sb1, L0_ffn_sw2, L0_ffn_sb2)
    x = x + _L0_attn_b_ref(_layernorm(x, axis=-1), L0_attn_b_A, L0_attn_b_B_w, L0_attn_b_B_b, L0_attn_b_C_w, L0_attn_b_C_b, L0_attn_b_D_w, L0_attn_b_D_b)
    x = x + _L0_ffn_ref(_layernorm(x, axis=-1), L0_ffn_router_w, L0_ffn_router_b, L0_ffn_w1, L0_ffn_b1, L0_ffn_w2, L0_ffn_b2, L0_ffn_sw1, L0_ffn_sb1, L0_ffn_sw2, L0_ffn_sb2)
    return x

_drawn_inputs = setup_inputs


def setup_inputs(seed=0):
    import zlib

    import numpy as np

    out = dict(_drawn_inputs(seed))
    spreads = {'L0_ffn_router_b': (0.0, 0.1),
     'L0_ffn_b1': (0.0, 0.8),
     'L0_ffn_b2': (0.0, 0.1),
     'L0_ffn_sb1': (0.0, 0.1),
     'L0_ffn_sb2': (0.0, 0.1)}
    factors = {'L0_attn_a_W_Q': 8.0,
     'L0_attn_a_W_K': 8.0,
     'L0_attn_a_W_V': 8.0,
     'L0_attn_b_A': 6.345,
     'L0_ffn_w1': 7.891,
     'L0_ffn_w2': 7.116}
    for name, (base, spread) in spreads.items():
        noise = np.random.default_rng([zlib.crc32(name.encode()), seed]).standard_normal(out[name].shape)
        drawn = base * np.exp(spread * noise) if base else spread * noise
        out[name] = jnp.asarray(drawn.astype(out[name].dtype))
    for name, factor in factors.items():
        out[name] = (out[name] * factor).astype(out[name].dtype)
    return out
```

```python
from contextlib import ExitStack

import numpy as np
import concourse.bass as bass
from concourse import mybir

F32 = mybir.dt.float32
F32R = mybir.dt.float32r
ALU = mybir.AluOpType
ACT = mybir.ActivationFunctionType
AX_X = mybir.AxisListType.X

P = 128
NB, L, D = 8, 512, 128
NE, HE = 64, 32
TC = 64
NC = L // TC
G = NB // 2
NS = 4
NR = NE * HE // P
NH = NS + NR
STATE = 32
LAG = 2
NSB = 4
EPS = 1e-5
GAMMA = 0.9
SCALE_BASE = 512.0
STEPS_PER_SLOT = 2
LOWEST = -3.0e38

SIDE = {
    "finish2": (3, NC + 2, 1, 0),
    "prepare2": (2, NC + 1, 2, 1),
    "finish1": (0, NC - 1, 1, 0),
    "prepare1": (-1, NC - 2, 3, 1),
    "scan_out": (1, NC, 0, 1),
    "scan_in": (0, NC - 1, 1, 2),
}
STEADY = (3, NC - 1)


def has(task, c):
    return not isinstance(c, int) or SIDE[task][0] <= c <= SIDE[task][1]


def before(task, c):
    lo, hi = SIDE[task][:2]
    return max(0, min(c - lo, hi - lo + 1)) if isinstance(c, int) else c - lo


def fills(bank, task, c):
    total = 0
    for name, row in SIDE.items():
        if row[2 + bank]:
            total = total + before(name, c) * row[2 + bank]
    for name, row in SIDE.items():
        if name == task:
            break
        if has(name, c):
            total = total + row[2 + bank]
    return total


def norms(task, c):
    order = ("prepare2", "prepare1", "scan_in")
    total = NB
    for name in order:
        total = total + before(name, c)
    for name in order[:order.index(task)]:
        if has(name, c):
            total = total + 1
    return total


def job(second, c):
    if not isinstance(c, int):
        return 2 * c - 2 + second
    first_before = max(0, min(c, NC))
    second_before = max(0, min(c - 2, NC))
    return first_before + second_before + (1 if second and 0 <= c < NC else 0)


def program(nc, X, Wqk, Wv, ropes, Dtab, ident, W1, W2, B1, B2, SB2, RW, RB, Sel, Acol, BwT, Bb, Ck,
            CD, DwT, out):
    ctx = ExitStack()
    with ctx:
        def sb(name, shape, dt=F32):
            return ctx.enter_context(nc.sbuf_tensor(name, shape, dt))

        def sem(name):
            return ctx.enter_context(nc.semaphore(name))

        ps = [ctx.enter_context(nc.psum_tensor(f"bank{i}", [P, 512], F32)) for i in range(8)]
        scores_ps, pT_ps, heads_ps = ps[0:2], ps[2:4], ps[4]
        proj_ps, side_ps = [ps[5], ps[7]], ps[6]
        hid_ps, gate_ps, y_ps, side = ps[0:2], ps[2:4], ps[4:6], ps[6:8]

        wqk = sb("wqk", [P, 4, D])
        wv = sb("wv", [P, D])
        rope = sb("rope", [P, 4, L])
        dtab = sb("dtab", [P, 4, L])
        idn = sb("idn", [P, P])
        w1raw = sb("w1raw", [P, NH * P])
        w1h = sb("w1h", [P, NH * P], F32R)
        w1l = sb("w1l", [P, NH * P], F32R)
        w2 = sb("w2", [P, NH, D])
        b1 = sb("b1", [P, NH])
        b2raw = sb("b2raw", [P, D])
        b2h = sb("b2h", [P, D], F32R)
        b2l = sb("b2l", [P, D], F32R)
        sb2 = sb("sb2", [P, 2])
        sb2sum = sb("sb2sum", [P, 1])
        rw = sb("rw", [P, NE])
        rb = sb("rb", [P, NE])
        selraw = sb("selraw", [P, NR * P])
        sel = sb("sel", [P, NR * P], F32R)
        acol = sb("acol", [P, 1])
        aexp = sb("aexp", [P, 1])
        bwT = sb("bwT", [P, STATE])
        bb = sb("bb", [P, 1])
        ck = sb("ck", [P, G, D])
        cd = sb("cd", [2, D])
        ones2 = sb("ones2", [2, P])
        dwT = sb("dwT", [P, D])
        mhalf = sb("mhalf", [P, 4])

        stats = sb("stats", [P, 4, 6])
        mv = sb("mv", [P, 4, 2])
        veps = sb("veps", [P, 4])
        rstd = sb("rstd", [P, 4])
        xn = sb("xn", [P, 4, D])
        xT = sb("xT", [P, 512])

        xin = sb("xin", [P, 4, D])
        rot = sb("rot", [P, 4, L])
        qT = sb("qT", [P, L])
        kT = sb("kT", [P, L])
        v = sb("v", [P, 4, D])
        nmax = sb("nmax", [P, 4])
        rsum = sb("rsum", [P, 4])
        rinv = sb("rinv", [P, 4])
        p = sb("p", [P, 2, L])
        pd = sb("pd", [P, 4, L])
        heads = sb("heads", [P, NB, L])

        xres = sb("xres", [P, G, D])
        headc = sb("headc", [P, NB, TC])
        x1 = sb("x1", [P, G, D])
        x2 = sb("x2", [P, G, D])
        x2d = sb("x2d", [P, G, D])
        x3 = sb("x3", [P, G, D])
        x3keep = sb("x3keep", [P, G, D])
        fin = sb("fin", [P, G, D])

        xh = [sb(f"xh{i}", [P, 512], F32R) for i in range(2)]
        xl = [sb(f"xl{i}", [P, 512], F32R) for i in range(2)]
        gateT = [sb(f"gateT{i}", [P, 512], F32R) for i in range(2)]
        lg = sb("lg", [P, 2, G, NE])
        top = sb("top", [P, G, 8])
        ex = sb("ex", [P, 2, G, NE])
        gsum = sb("gsum", [P, G])
        ginv = sb("ginv", [P, G])
        gate = sb("gate", [P, G, NE])
        gate2 = sb("gate2", [P, G, 2, NE])
        hid = sb("hid", [P, NSB, 512])
        yT = sb("yT", [P, 512])

        bu = sb("bu", [P, 2, TC])
        st = sb("st", [P, 2, TC])
        u = sb("u", [P, 2])

        w_attn = sem("w_attn")
        w_ffn = sem("w_ffn")
        consts_ready = sem("consts_ready")
        split_hi = sem("split_hi")
        split_done = sem("split_done")
        aexp_ready = sem("aexp_ready")
        x_in = sem("x_in")
        ln_step = sem("ln_step")
        rstd_ready = sem("rstd_ready")
        lnT_ps = sem("lnT_ps")
        xT_ready = sem("xT_ready")
        proj_done = sem("proj_done")
        rot_step = sem("rot_step")
        qk_ready = sem("qk_ready")
        v_ps = sem("v_ps")
        v_ready = sem("v_ready")
        scores_done = sem("scores_done")
        max_ready = sem("max_ready")
        exp_ready = sem("exp_ready")
        norm_step = sem("norm_step")
        pT_done = sem("pT_done")
        pd_ready = sem("pd_ready")
        av_done = sem("av_done")
        heads_ready = sem("heads_ready")

        xres_in = sem("xres_in")
        headc_ready = sem("headc_ready")
        filled = [sem("side0_filled"), sem("side1_filled")]
        emptied = [sem("side0_emptied"), sem("side1_emptied")]
        keep_ready = sem("keep_ready")
        xh_ready = sem("xh_ready")
        xl_ready = sem("xl_ready")
        route_step = sem("route_step")
        gexp_ready = sem("gexp_ready")
        hid_done = sem("hid_done")
        gateb_done = sem("gateb_done")
        silu_ready = sem("silu_ready")
        gated_ready = sem("gated_ready")
        used = sem("used")
        y_done = sem("y_done")
        yT_ready = sem("yT_ready")
        u_ready = sem("u_ready")
        st_ready = sem("st_ready")
        st_zero = sem("st_zero")
        stored = sem("stored")
        ROUTE = 9

        attn_loads = [(wqk[:], Wqk), (wv[:], Wv), (rope[:], ropes), (idn[:], ident), (dtab[:], Dtab)]
        ffn_loads = [(w1raw[:], W1), (w2[:], W2), (b1[:], B1), (b2raw[:], B2), (sb2[:], SB2), (rw[:], RW),
                     (rb[:], RB), (selraw[:], Sel), (acol[:], Acol), (bwT[:], BwT), (bb[:], Bb),
                     (ck[:], Ck), (cd[:], CD), (dwT[:], DwT)]
        ALL_ATTN, ALL_FFN = 16 * len(attn_loads), 16 * len(ffn_loads)

        x_by_batch = X.rearrange("b (k p) d -> b p k d", p=P)
        x_by_chunk = X.rearrange("(k g) (c t) d -> c g t k d", g=2, t=TC)
        out_by_chunk = out.rearrange("(k g) (c t) d -> c g t k d", g=2, t=TC)

        def iterations(eng, body):
            for c in range(-1, STEADY[0]):
                body(c)
            with eng.Fori(*STEADY) as c:
                body(c)
            for c in range(STEADY[1], NC + 3):
                body(c)

        FINISH = 2
        PREP = 3
        SCAN_OUT = 13
        SCAN_IN = 14

        def first_slot(c):
            return (0 <= c < NC) if isinstance(c, int) else True

        def second_slot(c):
            return (2 <= c < NC + 2) if isinstance(c, int) else True

        def scans(c):
            return (1 <= c <= NC) if isinstance(c, int) else True

        def slots(c, main, step, stages):
            for half in (0, 1):
                real = (first_slot, second_slot)[half](c)
                for j in range(NH):
                    at = half * NH + j
                    t = at * STEPS_PER_SLOT
                    if scans(c) and t < TC and step:
                        step(c, t)
                    if real and main:
                        main(half, c, j)
                    for s in range(t + 1, t + STEPS_PER_SLOT):
                        if scans(c) and s < TC and step:
                            step(c, s)
                    stages(half, c, j)

        def stage(half, c, j, task, at, where):
            first = {"finish2": 0, "prepare2": 0, "finish1": 1, "prepare1": 1, "scan_out": 1, "scan_in": 1}
            return half == first[task] and has(task, c) and j == at + where

        block = ctx.enter_context(nc.Block())

        def wait_apart(eng, semaphore, count):
            if not isinstance(count, int):
                count = eng.to_reg(count)
            eng.wait_ge(consts_ready, 1)
            eng.wait_ge(semaphore, count)

        @block.sync
        def _(sp):
            sp.dma_start(xin[:], x_by_batch[0]).then_inc(x_in, 16)
            for dst, src in attn_loads:
                sp.dma_start(dst, src).then_inc(w_attn, 16)
            with sp.Fori(1, NB) as b:
                sp.wait_ge(ln_step, 4 * b)
                sp.dma_start(xin[:], x_by_batch[bass.ds(b, 1)].rearrange("o p k d -> (o p) k d")).then_inc(x_in, 16)

            def body(c):
                if has("finish2", c):
                    sp.wait_ge(emptied[0], fills(0, "finish2", c) + 1)
                    for g in range(2):
                        dst = out_by_chunk[bass.ds(c - 3, 1), g].rearrange("o t k d -> (o t) k d")
                        sp.dma_start(dst, fin[g * TC:(g + 1) * TC]).then_inc(stored, 16)
                if has("prepare1", c):
                    if not isinstance(c, int) or c >= 0:
                        sp.wait_ge(emptied[0], fills(0, "prepare1", c - 1) + 1)
                    for g in range(2):
                        src = x_by_chunk[bass.ds(c + 1, 1), g].rearrange("o t k d -> (o t) k d")
                        sp.dma_start(xres[g * TC:(g + 1) * TC], src).then_inc(xres_in, 16)

            iterations(sp, body)
            sp.wait_ge(stored, 32 * NC)

        @block.gpsimd
        def _(pool):
            nc.gpsimd.memset(mhalf[:], -0.5)
            nc.gpsimd.memset(ones2[:], 1.0)
            nc.gpsimd.memset(st[:, :, TC - 1], 0.0).then_inc(consts_ready, 1)

            def inv_std(n):
                pool.wait_ge(ln_step, 4 * n + 3)
                nc.gpsimd.tensor_tensor(rstd[:], veps[:], mhalf[:], ALU.pow).then_inc(rstd_ready, 1)

            def rotated(b):
                for i, dst in enumerate((qT, kT)):
                    pool.wait_ge(rot_step, 4 * b + 2 * i + 2)
                    nc.gpsimd.tensor_tensor(dst[:], rot[:, 2 * i], rot[:, 2 * i + 1], ALU.add).then_inc(qk_ready, 1)

            pool.wait_ge(consts_ready, 1)
            inv_std(0)
            pool.wait_ge(w_ffn, ALL_FFN)
            nc.gpsimd.tensor_scalar(w1h[:], w1raw[:], 1.0, 0.0, ALU.mult, ALU.add)
            nc.gpsimd.tensor_scalar(b2h[:], b2raw[:], 1.0, 0.0, ALU.mult, ALU.add)
            nc.gpsimd.tensor_scalar(sel[:], selraw[:], 1.0, 0.0, ALU.mult, ALU.add).then_inc(split_hi, 1)
            rotated(0)
            with pool.Fori(1, NB) as b:
                inv_std(b)
                rotated(b)

            def stages(half, c, j):
                for i, task in enumerate(("prepare1", "prepare2")):
                    if stage(half, c, j, task, PREP, 1):
                        inv_std(norms(task, c))
                    if stage(half, c, j, task, PREP, 4):
                        wait_apart(pool, emptied[0], fills(0, task, c) + (2 if i == 0 else 1))
                        nc.gpsimd.tensor_scalar(xh[i][:], xT[:], 1.0, 0.0, ALU.mult, ALU.add).then_inc(xh_ready, 1)
                if stage(half, c, j, "scan_in", SCAN_IN, 0):
                    inv_std(norms("scan_in", c))

            iterations(pool, lambda c: slots(c, None, None, stages))

        @block.scalar
        def _(act):
            def attend_exp(b, i):
                act.wait_ge(max_ready, 4 * b + i + 1)
                if i >= 2 or not isinstance(b, int) or b > 0:
                    act.wait_ge(pT_done, 4 * b + i - 1)
                nc.scalar.activation(p[:, i % 2], scores_ps[i % 2][:], ACT.Exp, bias=nmax[:, i:i + 1],
                                     accum_out=rsum[:, i:i + 1]).then_inc(exp_ready, 1)

            def copy_xT(b):
                act.wait_ge(lnT_ps, b + 1)
                nc.scalar.copy(xT[:], side_ps[:]).then_inc(xT_ready, 1)

            def copy_v(b):
                act.wait_ge(v_ps, b + 1)
                nc.scalar.copy(v[:].rearrange("p k d -> p (k d)"), side_ps[:]).then_inc(v_ready, 1)

            def copy_heads(b):
                act.wait_ge(av_done, b + 1)
                dst = heads[:, bass.ds(b, 1)].rearrange("p o t -> p (o t)")
                nc.scalar.copy(dst, heads_ps[:]).then_inc(heads_ready, 1)

            for dst, src in ffn_loads:
                act.dma_start(dst, src).then_inc(w_ffn, 16)
            copy_xT(0)
            copy_v(0)

            def attention(b, more):
                for i in range(4):
                    attend_exp(b, i)
                if more:
                    copy_xT(b + 1)
                copy_heads(b)
                if more:
                    copy_v(b + 1)

            attention(0, True)
            with act.Fori(1, NB - 1) as b:
                attention(b, True)
            attention(NB - 1, False)
            act.wait_ge(w_ffn, ALL_FFN)
            nc.scalar.activation(aexp[:], acol[:], ACT.Exp).then_inc(aexp_ready, 1)

            def main(half, c, j):
                n = job(half, c) * NH + j
                act.wait_ge(hid_done, n + 1)
                if not isinstance(n, int) or n >= NSB:
                    act.wait_ge(used, n - NSB + 1)
                nc.scalar.activation(hid[:, j % NSB], hid_ps[j % 2][:], ACT.Silu, bias=b1[:, j:j + 1]).then_inc(silu_ready, 1)

            def step(c, t):
                act.wait_ge(u_ready, (c - 1) * TC + t + 1)
                nc.scalar.activation(st[:, :, t], u[:], ACT.Tanh).then_inc(st_ready, 1)

            def stages(half, c, j):
                for i, task in enumerate(("finish1", "finish2")):
                    if stage(half, c, j, task, FINISH, 0):
                        n = job(0, c) if i == 0 else job(1, c - 1)
                        act.wait_ge(y_done, n + 1)
                        nc.scalar.activation(yT[:], y_ps[i][:], ACT.Identity, bias=sb2sum[:]).then_inc(yT_ready, 1)
                for i, task in enumerate(("prepare1", "prepare2")):
                    first = 1 if i == 0 else 0
                    if i == 0 and stage(half, c, j, task, PREP, 0):
                        if isinstance(c, int) and c < 0:
                            act.wait_ge(heads_ready, NB)
                        else:
                            act.wait_ge(filled[0], fills(0, task, c - 1) + 1)
                        src = heads[:, :, bass.ds((c + 1) * TC, TC)]
                        nc.scalar.copy(headc[:], src).then_inc(headc_ready, 1)
                    if stage(half, c, j, task, PREP, 3):
                        act.wait_ge(filled[0], fills(0, task, c) + first + 1)
                        nc.scalar.copy(xT[:], side[0][:]).then_inc(emptied[0], 1)
                    if stage(half, c, j, task, PREP, 6):
                        act.wait_ge(route_step, job(i, c + 1 - i) * ROUTE + 3)
                        nc.scalar.activation(ex[:], lg[:], ACT.Exp).then_inc(gexp_ready, 1)
                    if stage(half, c, j, task, PREP, 8):
                        act.wait_ge(filled[0], fills(0, task, c) + first + 2)
                        nc.scalar.copy(gateT[i][:], side[0][:]).then_inc(emptied[0], 1)
                if stage(half, c, j, "scan_in", SCAN_IN, 2):
                    act.wait_ge(filled[0], fills(0, "scan_in", c) + 1)
                    nc.scalar.copy(xT[:], side[0][:]).then_inc(emptied[0], 1)

            iterations(act, lambda c: slots(c, main, step, stages))

        @block.vector
        def _(dve):
            def ln_stats(n, x):
                for k in range(4):
                    last = nc.vector.bn_stats(stats[:, k], x[:, k])
                last.then_inc(ln_step, 1)
                wait_apart(dve, ln_step, 4 * n + 1)
                for k in range(4):
                    last = nc.vector.bn_aggr(mv[:, k], stats[:, k])
                last.then_inc(ln_step, 1)
                dve.wait_ge(ln_step, 4 * n + 2)
                nc.vector.tensor_scalar(veps[:], mv[:, :, 1], EPS, None, ALU.add).then_inc(ln_step, 1)

            def ln_apply(n, x):
                dve.wait_ge(rstd_ready, n + 1)
                for k in range(4):
                    last = nc.vector.tensor_scalar(xn[:, k], x[:, k], mv[:, k, 0:1], rstd[:, k:k + 1],
                                                   ALU.subtract, ALU.mult)
                last.then_inc(ln_step, 1)

            def rotate(b, i):
                dve.wait_ge(proj_done, 2 * b + i + 1)
                if not isinstance(b, int) or b > 0:
                    dve.wait_ge(qk_ready, 2 * b + i - 1)
                for h in range(2):
                    nc.vector.tensor_tensor(rot[:, 2 * i + h], proj_ps[h][:], rope[:, 2 * i + h], ALU.mult).then_inc(rot_step, 1)

            def neg_max(b, i):
                dve.wait_ge(scores_done, 4 * b + i + 1)
                nc.vector.tensor_reduce(nmax[:, i:i + 1], scores_ps[i % 2][:], AX_X, ALU.max, negate=True).then_inc(max_ready, 1)

            def normalise(b, i):
                dve.wait_ge(exp_ready, 4 * b + i + 1)
                nc.vector.reciprocal(rinv[:, i:i + 1], rsum[:, i:i + 1]).then_inc(norm_step, 1)
                dve.wait_ge(norm_step, 8 * b + 2 * i + 1)
                nc.vector.tensor_scalar(p[:, i % 2], p[:, i % 2], rinv[:, i:i + 1], None, ALU.mult).then_inc(norm_step, 1)

            def decay(b, i):
                dve.wait_ge(pT_done, 4 * b + i + 1)
                if i == 0 and (not isinstance(b, int) or b > 0):
                    dve.wait_ge(av_done, b)
                cols = slice(i * P, (i + 1) * P)
                nc.vector.tensor_tensor(pd[:, :, cols], pT_ps[i % 2][:].rearrange("p (k q) -> p k q", k=4),
                                        dtab[:, :, cols], ALU.mult).then_inc(pd_ready, 1)

            def attention(b, more):
                neg_max(b, 0)
                neg_max(b, 1)
                if more:
                    dve.wait_ge(x_in, 16 * (b + 2))
                    ln_stats(b + 1, xin)
                neg_max(b, 2)
                normalise(b, 0)
                neg_max(b, 3)
                normalise(b, 1)
                if more:
                    ln_apply(b + 1, xin)
                decay(b, 0)
                normalise(b, 2)
                decay(b, 1)
                normalise(b, 3)
                if more:
                    rotate(b + 1, 0)
                decay(b, 2)
                decay(b, 3)
                if more:
                    rotate(b + 1, 1)

            dve.wait_ge(x_in, 16)
            ln_stats(0, xin)
            ln_apply(0, xin)
            dve.wait_ge(w_attn, ALL_ATTN)
            rotate(0, 0)
            rotate(0, 1)
            dve.wait_ge(split_hi, 1)
            nc.vector.tensor_tensor(w1l[:], w1raw[:], w1h[:].bitcast(F32), ALU.subtract)
            nc.vector.tensor_tensor(b2l[:], b2raw[:], b2h[:].bitcast(F32), ALU.subtract)
            nc.vector.tensor_tensor(sb2sum[:], sb2[:, 0:1], sb2[:, 1:2], ALU.add).then_inc(split_done, 1)
            attention(0, True)
            with dve.Fori(1, NB - 1) as b:
                attention(b, True)
            attention(NB - 1, False)
            dve.wait_ge(aexp_ready, 1)

            def main(half, c, j):
                if j < NS:
                    return
                n = job(half, c) * NH + j
                r = job(half, c) * NR + j - NS
                dve.wait_ge(silu_ready, n + 1)
                dve.wait_ge(gateb_done, r + 1)
                nc.vector.tensor_tensor(hid[:, j % NSB], gate_ps[j % 2][:], hid[:, j % NSB], ALU.mult).then_inc(gated_ready, 1)

            def step(c, t):
                s = (c - 1) * TC + t
                if t == 0:
                    dve.wait_ge(emptied[1], fills(1, "scan_in", c - 1) + 1)
                if not isinstance(s, int) or s > 0:
                    dve.wait_ge(st_ready, s)
                nc.vector.scalar_tensor_tensor(u[:], st[:, :, (t - 1) % TC], aexp[:], bu[:, :, t],
                                               ALU.mult, ALU.add).then_inc(u_ready, 1)

            def flat(x):
                return x[:].rearrange("p k d -> p (k d)")

            def spread(cols, n):
                return cols.broadcast_to([P, G, n])

            def stages(half, c, j):
                for i, task in enumerate(("finish1", "finish2")):
                    if stage(half, c, j, task, FINISH, 0):
                        dve.wait_ge(filled[0], fills(0, task, c) + 1)
                        if i == 0:
                            nc.vector.tensor_tensor(flat(x2), side[0][:], flat(x1), ALU.add).then_inc(emptied[0], 1)
                        else:
                            if not isinstance(c, int) or c > 3:
                                dve.wait_ge(stored, 32 * (c - 3))
                            nc.vector.tensor_tensor(flat(fin), side[0][:], flat(x3keep), ALU.add).then_inc(emptied[0], 1)
                for i, task in enumerate(("prepare1", "prepare2")):
                    x = (x1, x3keep)[i]
                    u1 = fills(1, task, c)
                    if stage(half, c, j, task, PREP, 1):
                        if i == 0:
                            u0 = fills(0, task, c)
                            dve.wait_ge(filled[0], u0 + 1)
                            dve.wait_ge(xres_in, 32 * (c + 2))
                            if has("finish1", c):
                                dve.wait_ge(emptied[0], fills(0, "finish1", c) + 1)
                            nc.vector.tensor_tensor(flat(x1), side[0][:], flat(xres), ALU.add).then_inc(emptied[0], 1)
                            dve.wait_ge(emptied[0], u0 + 1)
                        else:
                            dve.wait_ge(emptied[1], fills(1, "scan_out", c - 1) + 1)
                            if has("finish2", c):
                                dve.wait_ge(emptied[0], fills(0, "finish2", c) + 1)
                            nc.vector.tensor_copy(flat(x3keep), flat(x3)).then_inc(keep_ready, 1)
                            dve.wait_ge(keep_ready, c - 1)
                        ln_stats(norms(task, c), x)
                    if stage(half, c, j, task, PREP, 2):
                        ln_apply(norms(task, c), x)
                    q = job(i, c + 1 - i)
                    r = q * ROUTE
                    if stage(half, c, j, task, PREP, 4):
                        dve.wait_ge(filled[1], u1 + 1)
                        nc.vector.tensor_tensor(lg[:, 0], side[1][:, 0:G * NE].rearrange("p (k e) -> p k e", k=G),
                                                rb[:].rearrange("p (o e) -> p o e", o=1).broadcast_to([P, G, NE]),
                                                ALU.add).then_inc(emptied[1], 1)
                        wait_apart(dve, emptied[1], u1 + 1)
                        for k in range(G):
                            last = nc.vector.max(top[:, k], lg[:, 0, k])
                        last.then_inc(route_step, 1)
                        wait_apart(dve, route_step, r + 1)
                        for k in range(G):
                            last = nc.vector.match_replace(lg[:, 1, k], top[:, k], lg[:, 0, k], LOWEST)
                        last.then_inc(route_step, 1)
                        dve.wait_ge(route_step, r + 2)
                        for h in range(2):
                            last = nc.vector.tensor_tensor(lg[:, h], lg[:, h], spread(top[:, :, 0:1], NE), ALU.subtract)
                        last.then_inc(route_step, 1)
                        dve.wait_ge(xh_ready, q + 1)
                        nc.vector.tensor_tensor(xl[i][:], xT[:], xh[i][:].bitcast(F32), ALU.subtract).then_inc(xl_ready, 1)
                    if stage(half, c, j, task, PREP, 7):
                        dve.wait_ge(gexp_ready, q + 1)
                        nc.vector.tensor_tensor(gate[:], ex[:, 0], ex[:, 1], ALU.subtract).then_inc(route_step, 1)
                        dve.wait_ge(route_step, r + 4)
                        nc.vector.tensor_reduce(gsum[:], gate[:], AX_X, ALU.add).then_inc(route_step, 1)
                        dve.wait_ge(route_step, r + 5)
                        nc.vector.reciprocal(ginv[:], gsum[:]).then_inc(route_step, 1)
                        dve.wait_ge(route_step, r + 6)
                        nc.vector.tensor_tensor(gate[:], gate[:], spread(ginv[:].rearrange("p (k o) -> p k o", o=1), NE), ALU.mult).then_inc(route_step, 1)
                        dve.wait_ge(route_step, r + 7)
                        nc.vector.tensor_copy(gate2[:, :, 0].bitcast(F32R), gate[:]).then_inc(route_step, 1)
                        dve.wait_ge(route_step, r + 8)
                        nc.vector.tensor_tensor(gate2[:, :, 1].bitcast(F32R), gate[:], gate2[:, :, 0], ALU.subtract).then_inc(route_step, 1)
                if stage(half, c, j, "scan_out", SCAN_OUT, 0):
                    dve.wait_ge(filled[1], fills(1, "scan_out", c) + 1)
                    nc.vector.tensor_tensor(flat(x3), side[1][:], flat(x2d), ALU.add).then_inc(emptied[1], 1)
                if stage(half, c, j, "scan_in", SCAN_IN, 0):
                    dve.wait_ge(emptied[0], fills(0, "finish1", c) + 1)
                    ln_stats(norms("scan_in", c), x2)
                if stage(half, c, j, "scan_in", SCAN_IN, 1):
                    ln_apply(norms("scan_in", c), x2)
                if stage(half, c, j, "scan_in", SCAN_IN, 3):
                    dve.wait_ge(filled[1], fills(1, "scan_in", c) + 1)
                    nc.vector.tensor_scalar(bu[:].rearrange("p g t -> p (g t)"), side[1][:, 0:2 * TC], bb[:], None,
                                            ALU.add).then_inc(emptied[1], 1)
                if stage(half, c, j, "scan_in", SCAN_IN, 4):
                    dve.wait_ge(filled[1], fills(1, "scan_in", c) + 2)
                    nc.vector.tensor_tensor(flat(x2d), side[1][:], flat(x2), ALU.add).then_inc(emptied[1], 1)

            iterations(dve, lambda c: slots(c, main, step, stages))

        @block.tensor
        def _(pe):
            def transpose4(dst, parts):
                for k in range(4):
                    last = nc.tensor.transpose(dst[:, k * P:(k + 1) * P], parts(k), idn[:])
                return last

            def transposed_x(b):
                pe.wait_ge(ln_step, 4 * b + 4)
                if not isinstance(b, int) or b > 0:
                    pe.wait_ge(v_ready, b)
                transpose4(side_ps, lambda k: xn[:, k]).then_inc(lnT_ps, 1)

            def project(b, i):
                if i == 0:
                    pe.wait_ge(xT_ready, b + 1)
                if not isinstance(b, int) or b > 0 or i > 0:
                    pe.wait_ge(rot_step, 4 * b + 2 * i)
                for h in range(2):
                    last = nc.tensor.matmul(proj_ps[h][:], wqk[:, 2 * i + h], xT[:], start=True, stop=True)
                last.then_inc(proj_done, 1)

            def values(b):
                pe.wait_ge(xT_ready, b + 1)
                for k in range(4):
                    last = nc.tensor.matmul(side_ps[:, k * P:(k + 1) * P], xT[:, k * P:(k + 1) * P], wv[:],
                                            start=True, stop=True)
                last.then_inc(v_ps, 1)

            def score(b, i):
                if i == 0:
                    pe.wait_ge(qk_ready, 2 * b + 2)
                if i >= 2:
                    pe.wait_ge(exp_ready, 4 * b + i - 1)
                nc.tensor.matmul(scores_ps[i % 2][:], qT[:, i * P:(i + 1) * P], kT[:], start=True, stop=True).then_inc(scores_done, 1)

            def weights(b, i):
                pe.wait_ge(norm_step, 8 * b + 2 * i + 2)
                if i >= 2:
                    pe.wait_ge(pd_ready, 4 * b + i - 1)
                transpose4(pT_ps[i % 2], lambda k: p[:, i % 2, k * P:(k + 1) * P]).then_inc(pT_done, 1)

            def attend(b):
                pe.wait_ge(pd_ready, 4 * b + 4)
                pe.wait_ge(v_ready, b + 1)
                if not isinstance(b, int) or b > 0:
                    pe.wait_ge(heads_ready, b)
                for k in range(4):
                    last = nc.tensor.matmul(heads_ps[:], v[:, k], pd[:, k], start=(k == 0), stop=(k == 3))
                last.then_inc(av_done, 1)

            def attention(b, more):
                for i in range(4):
                    score(b, i)
                weights(b, 0)
                weights(b, 1)
                if more:
                    transposed_x(b + 1)
                    project(b + 1, 0)
                weights(b, 2)
                weights(b, 3)
                if more:
                    project(b + 1, 1)
                attend(b)
                if more:
                    values(b + 1)

            pe.wait_ge(w_attn, ALL_ATTN)
            transposed_x(0)
            project(0, 0)
            project(0, 1)
            values(0)
            attention(0, True)
            with pe.Fori(1, NB - 1) as b:
                attention(b, True)
            attention(NB - 1, False)
            pe.wait_ge(split_done, 1)
            pe.wait_ge(consts_ready, 1)

            def second_product(half, c, j):
                q = job(half, c)
                if j < NS:
                    pe.wait_ge(silu_ready, q * NH + j + 1)
                else:
                    pe.wait_ge(gated_ready, q * NR + j - NS + 1)
                nc.tensor.matmul(y_ps[half][:], w2[:, j], hid[:, j % NSB], start=(j == 0), stop=False).then_inc(used, 1)
                if j == NH - 1:
                    nc.tensor.matmul(y_ps[half][:], b2l[:], gateT[half][:], start=False, stop=False)
                    nc.tensor.matmul(y_ps[half][:], b2h[:], gateT[half][:], start=False, stop=True).then_inc(y_done, 1)

            def main(half, c, j):
                q = job(half, c)
                n = q * NH + j
                r = q * NR + j - NS
                if j == 0:
                    pe.wait_ge(xl_ready, q + 1)
                if not isinstance(n, int) or n >= 2:
                    pe.wait_ge(silu_ready, n - 1)
                cols = slice(j * P, (j + 1) * P)
                nc.tensor.matmul(hid_ps[j % 2][:], w1l[:, cols], xh[half][:], start=True, stop=False)
                nc.tensor.matmul(hid_ps[j % 2][:], w1h[:, cols], xl[half][:], start=False, stop=False)
                nc.tensor.matmul(hid_ps[j % 2][:], w1h[:, cols], xh[half][:], start=False, stop=True).then_inc(hid_done, 1)
                if j >= NS:
                    if j == NS:
                        task, at = (("prepare1", c - 1), ("prepare2", c))[half]
                        pe.wait_ge(emptied[0], fills(0, task, at) + (3 if half == 0 else 2))
                    if not isinstance(r, int) or r >= 2:
                        pe.wait_ge(gated_ready, r - 1)
                    g = j - NS
                    nc.tensor.matmul(gate_ps[j % 2][:], sel[:, g * P:(g + 1) * P], gateT[half][:],
                                     start=True, stop=True).then_inc(gateb_done, 1)
                if j >= LAG:
                    second_product(half, c, j - LAG)

            def fill(bank, task, c, k):
                n = fills(bank, task, c) + k
                if not isinstance(n, int) or n > 0:
                    pe.wait_ge(emptied[bank], n)

            def stages(half, c, j):
                before_c = c if half else c - 1
                if (first_slot if half else second_slot)(before_c) and j < LAG:
                    if not (isinstance(before_c, int) and before_c < 0):
                        second_product(1 - half, before_c, NH - LAG + j)
                for i, task in enumerate(("finish1", "finish2")):
                    if stage(half, c, j, task, FINISH, 0):
                        pe.wait_ge(yT_ready, (job(0, c) if i == 0 else job(1, c - 1)) + 1)
                        fill(0, task, c, 0)
                        transpose4(side[0], lambda k: yT[:, k * P:(k + 1) * P]).then_inc(filled[0], 1)
                for i, task in enumerate(("prepare1", "prepare2")):
                    k0 = 1 if i == 0 else 0
                    if i == 0 and stage(half, c, j, task, PREP, 1):
                        pe.wait_ge(headc_ready, c + 2)
                        fill(0, task, c, 0)
                        transpose4(side[0], lambda k: headc[:, 2 * k:2 * k + 2].rearrange("p g t -> p (g t)")).then_inc(filled[0], 1)
                    if stage(half, c, j, task, PREP, 3):
                        pe.wait_ge(ln_step, 4 * norms(task, c) + 4)
                        fill(0, task, c, k0)
                        transpose4(side[0], lambda k: xn[:, k]).then_inc(filled[0], 1)
                    if stage(half, c, j, task, PREP, 4):
                        pe.wait_ge(emptied[0], fills(0, task, c) + k0 + 1)
                        fill(1, task, c, 0)
                        for k in range(G):
                            last = nc.tensor.matmul(side[1][:, k * NE:(k + 1) * NE], xT[:, k * P:(k + 1) * P], rw[:],
                                                    start=True, stop=True)
                        last.then_inc(filled[1], 1)
                    if stage(half, c, j, task, PREP, 8):
                        pe.wait_ge(route_step, (job(i, c + 1 - i) + 1) * ROUTE)
                        fill(0, task, c, k0 + 1)
                        transpose4(side[0], lambda k: gate2[:, k].rearrange("p h e -> p (h e)")).then_inc(filled[0], 1)
                if stage(half, c, j, "scan_out", SCAN_OUT, 0):
                    pe.wait_ge(st_ready, c * TC)
                    fill(1, "scan_out", c, 0)
                    for k in range(G):
                        last = nc.tensor.matmul(side[1][:, k * P:(k + 1) * P], st[:].rearrange("p g t -> p (g t)"),
                                                ck[:, k], start=True, stop=True)
                    last.then_inc(filled[1], 1)
                if stage(half, c, j, "scan_in", SCAN_IN, 2):
                    pe.wait_ge(ln_step, 4 * norms("scan_in", c) + 4)
                    fill(0, "scan_in", c, 0)
                    transpose4(side[0], lambda k: xn[:, k]).then_inc(filled[0], 1)
                if stage(half, c, j, "scan_in", SCAN_IN, 3):
                    pe.wait_ge(emptied[0], fills(0, "scan_in", c) + 1)
                    fill(1, "scan_in", c, 0)
                    for k in range(G):
                        last = nc.tensor.matmul(side[1][k * STATE:(k + 1) * STATE, 0:P], bwT[:], xT[:, k * P:(k + 1) * P],
                                                start=True, stop=True)
                    last.then_inc(filled[1], 1)
                if stage(half, c, j, "scan_in", SCAN_IN, 4):
                    fill(1, "scan_in", c, 1)
                    for k in range(G):
                        dst = side[1][:, k * P:(k + 1) * P]
                        nc.tensor.matmul(dst, xT[:, k * P:(k + 1) * P], dwT[:], start=True, stop=False)
                        last = nc.tensor.matmul(dst, ones2[:], cd[:], start=False, stop=True)
                    last.then_inc(filled[1], 1)

            iterations(pe, lambda c: slots(c, main, None, stages))


def tables():
    half = D // 2
    f = np.float32
    scale_vec = (np.arange(0, D, 2, dtype=f) + f(0.4 * D)) / f(1.4 * D)
    power = np.arange(L, dtype=f) / f(SCALE_BASE)
    scale = (scale_vec[None, :] ** power[:, None]).astype(f)
    inv_freq = (f(1.0) / f(10000.0) ** (np.arange(half, dtype=f) / f(half))).astype(f)
    angle = np.arange(L, dtype=f)[:, None] * inv_freq[None, :]
    sign = np.where(np.arange(D) % 2 == 0, f(-1), f(1))[None, :]
    rows = []
    for s in (scale, f(1.0) / scale):
        rows.append(np.repeat(np.cos(angle) * s, 2, axis=-1).T)
        rows.append((np.repeat(np.sin(angle) * s, 2, axis=-1) * sign).T)
    ropes = np.ascontiguousarray(np.stack(rows, axis=1), dtype=f)
    k = np.arange(L).reshape(4, P).T[:, :, None]
    decay = (GAMMA ** np.abs(k - np.arange(L)[None, None, :])).astype(f)
    sel = np.zeros((P, NR, P), f)
    for j in range(NR):
        for m in range(P):
            e = j * (P // HE) + m // HE
            sel[e, j, m] = sel[NE + e, j, m] = 1.0
    return ropes, decay, np.eye(P, dtype=f), sel.reshape(P, NR * P)


def kernel(**inputs):
    import concourse.bacc as bacc
    from concourse.bass_utils import run_bass_kernel_spmd

    a = {k.replace("L0_", ""): np.asarray(v) for k, v in inputs.items()}
    swap = np.arange(D) ^ 1
    wq, wk = a["attn_a_W_Q"], a["attn_a_W_K"]
    ropes, decay, eye, sel = tables()
    ck = np.zeros((P, G, D), np.float32)
    for k in range(G):
        ck[k * STATE:(k + 1) * STATE, k] = a["attn_b_C_w"].T
    w1 = np.concatenate([a["ffn_sw1"].transpose(1, 0, 2).reshape(D, NS * P),
                         a["ffn_w1"].transpose(1, 0, 2).reshape(D, NR * P)], axis=1)
    w2 = np.concatenate([a["ffn_sw2"].reshape(NS, P, D), a["ffn_w2"].reshape(NR, P, D)]).transpose(1, 0, 2)
    b1 = np.concatenate([a["ffn_sb1"].reshape(NS, P), a["ffn_b1"].reshape(NR, P)]).T
    arrays = {
        "X": a["attn_a_X"],
        "Wqk": np.stack([wq, wq[:, swap], wk, wk[:, swap]], axis=1),
        "Wv": a["attn_a_W_V"], "ropes": ropes, "Dtab": decay, "ident": eye,
        "W1": w1, "W2": w2, "B1": b1, "B2": np.concatenate([a["ffn_b2"]] * 2), "SB2": a["ffn_sb2"].T,
        "RW": a["ffn_router_w"], "RB": np.tile(a["ffn_router_b"][None], (P, 1)), "Sel": sel,
        "Acol": np.tile(a["attn_b_A"], G)[:, None], "BwT": a["attn_b_B_w"].T,
        "Bb": np.tile(a["attn_b_B_b"], G)[:, None], "Ck": ck,
        "CD": np.stack([a["attn_b_C_b"], a["attn_b_D_b"]]), "DwT": a["attn_b_D_w"].T,
    }
    arrays = {k: np.ascontiguousarray(x) for k, x in arrays.items()}
    nc = bacc.Bacc("TRN2", target_bir_lowering=False, num_devices=1)
    aps = [nc.dram_tensor(k, x.shape, F32, kind="ExternalInput").ap() for k, x in arrays.items()]
    out = nc.dram_tensor("out", (NB, L, D), F32, kind="ExternalOutput").ap()
    program(nc, *aps, out)
    r = run_bass_kernel_spmd(nc, [arrays], core_ids=[0])
    return r.results[0]["out"]
```

```python
from contextlib import ExitStack

import numpy as np
import concourse.bass as bass
from concourse import mybir

F32 = mybir.dt.float32
F32R = mybir.dt.float32r
ALU = mybir.AluOpType
ACT = mybir.ActivationFunctionType
AX_X = mybir.AxisListType.X

P = 128
NB, L, D = 8, 512, 128
NE, HE = 64, 32
TC = 64
NC = L // TC
G = NB // 2
NS = 4
NR = NE * HE // P
NH = NS + NR
STATE = 32
LAG = 3
NSB = 4
EPS = 1e-5
GAMMA = 0.9
SCALE_BASE = 512.0
STEPS_PER_SLOT = 2
LOWEST = -3.0e38

SIDE = {
    "finish2": (3, NC + 2),
    "prepare2": (2, NC + 1),
    "finish1": (0, NC - 1),
    "prepare1": (-1, NC - 2),
    "scan_out": (1, NC),
    "scan_in": (0, NC - 1),
}
STEADY = (3, NC - 1)
FILLS = (
    (("finish2", "y"), ("prepare2", "x"), ("prepare2", "gate"), ("finish1", "y"), ("prepare1", "x"),
     ("scan_in", "x"), ("prepare1", "gate")),
    (("prepare2", "logits"), ("prepare1", "heads"), ("prepare1", "logits"), ("scan_out", "y"),
     ("scan_in", "bu"), ("scan_in", "direct")),
)
NORMS = (("prepare2", "x"), ("prepare1", "x"))


def has(task, c):
    return not isinstance(c, int) or SIDE[task][0] <= c <= SIDE[task][1]


def before(task, c):
    lo, hi = SIDE[task]
    return max(0, min(c - lo, hi - lo + 1)) if isinstance(c, int) else c - lo


def count(order, task, what, c):
    total = 0
    for name, _ in order:
        total = total + before(name, c)
    for name, _ in order[:order.index((task, what))]:
        if has(name, c):
            total = total + 1
    return total


def fills(bank, task, what, c):
    return count(FILLS[bank], task, what, c)


def norms(task, c):
    return before(task, c) if task == "scan_in" else NB + count(NORMS, task, "x", c)


def job(second, c):
    if not isinstance(c, int):
        return 2 * c - 2 + second
    first_before = max(0, min(c, NC))
    second_before = max(0, min(c - 2, NC))
    return first_before + second_before + (1 if second and 0 <= c < NC else 0)


def program(nc, X, Wqk, Wv, ropes, Dtab, ident, W1, W2, B1, B2, SB2, RW, RB, Sel, Acol, BwT, Bb, Ck,
            CD, DwT, out):
    ctx = ExitStack()
    with ctx:
        def sb(name, shape, dt=F32):
            return ctx.enter_context(nc.sbuf_tensor(name, shape, dt))

        def sem(name):
            return ctx.enter_context(nc.semaphore(name))

        ps = [ctx.enter_context(nc.psum_tensor(f"bank{i}", [P, 512], F32)) for i in range(8)]
        scores_ps, pT_ps, heads_ps = ps[0:2], ps[2:4], ps[4]
        proj_ps, side_ps = [ps[5], ps[7]], ps[6]
        hid_ps, gate_ps, y_ps, side = ps[0:2], ps[2:4], ps[4:6], ps[6:8]

        wqk = sb("wqk", [P, 4, D])
        wv = sb("wv", [P, D])
        rope = sb("rope", [P, 4, L])
        dtab = sb("dtab", [P, 3 * P + L])
        idn = sb("idn", [P, P])
        w1raw = sb("w1raw", [P, NH * P])
        w1h = sb("w1h", [P, NH * P], F32R)
        w1l = sb("w1l", [P, NH * P], F32R)
        w2 = sb("w2", [P, NH, D])
        b1 = sb("b1", [P, NH])
        b2raw = sb("b2raw", [P, D])
        b2h = sb("b2h", [P, D], F32R)
        b2l = sb("b2l", [P, D], F32R)
        sb2 = sb("sb2", [P, 2])
        sb2sum = sb("sb2sum", [P, 1])
        rw = sb("rw", [P, NE])
        rb = sb("rb", [P, NE])
        selraw = sb("selraw", [P, NR * P])
        sel = sb("sel", [P, NR * P], F32R)
        acol = sb("acol", [P, 1])
        aexp = sb("aexp", [P, 1])
        bwT = sb("bwT", [P, STATE])
        bb = sb("bb", [P, 1])
        ck = sb("ck", [P, G, D])
        cd = sb("cd", [2, D])
        ones2 = sb("ones2", [2, P])
        dwT = sb("dwT", [P, D])
        mhalf = sb("mhalf", [P, 4])

        stats = [sb(f"stats{i}", [P, 4, 6]) for i in range(2)]
        mv = [sb(f"mv{i}", [P, 4, 2]) for i in range(2)]
        veps = [sb(f"veps{i}", [P, 4]) for i in range(2)]
        rstd = [sb(f"rstd{i}", [P, 4]) for i in range(2)]
        xn = sb("xn", [P, 4, D])
        xT = sb("xT", [P, 512])
        xns = sb("xns", [P, 4, D])
        xTs = sb("xTs", [P, 512])

        xin = sb("xin", [P, 4, D])
        rot = sb("rot", [P, 4, L])
        qT = sb("qT", [P, L])
        kT = sb("kT", [P, L])
        v = sb("v", [P, 4, D])
        nmax = sb("nmax", [P, 4])
        rsum = sb("rsum", [P, 4])
        rinv = sb("rinv", [P, 4])
        p = sb("p", [P, 2, L])
        pd = sb("pd", [P, 4, L])
        heads = sb("heads", [P, NB, L])

        xres = sb("xres", [P, G, D])
        headc = sb("headc", [P, NB, TC])
        x1 = sb("x1", [P, G, D])
        x1keep = sb("x1keep", [P, G, D])
        x2 = sb("x2", [P, G, D])
        x2d = sb("x2d", [P, G, D])
        x3 = sb("x3", [P, G, D])
        x3keep = sb("x3keep", [P, G, D])
        fin = sb("fin", [P, G, D])

        xh = [sb(f"xh{i}", [P, 512], F32R) for i in range(2)]
        xl = [sb(f"xl{i}", [P, 512], F32R) for i in range(2)]
        gateT = [sb(f"gateT{i}", [P, 512], F32R) for i in range(2)]
        lg = sb("lg", [P, 2, G, NE])
        top = sb("top", [P, G, 8])
        th = sb("th", [P, G, NE])
        den = sb("den", [P, G, NE])
        gsum = sb("gsum", [P, G])
        ginv = sb("ginv", [P, G])
        gate = sb("gate", [P, G, NE])
        gate2 = sb("gate2", [P, G, 2, NE])
        hid = sb("hid", [P, NSB, 512])
        yT = sb("yT", [P, 512])

        bu = sb("bu", [P, 2, TC])
        st = sb("st", [P, 2, TC])
        u = sb("u", [P, 2])

        w_proj = sem("w_proj")
        w_rope = sem("w_rope")
        w_decay = sem("w_decay")
        w_ident = sem("w_ident")
        w_ffn = sem("w_ffn")
        consts_ready = sem("consts_ready")
        split_hi = sem("split_hi")
        split_done = sem("split_done")
        aexp_ready = sem("aexp_ready")
        x_in = sem("x_in")
        ln_step = [sem("ln_step"), sem("scan_ln_step")]
        rstd_ready = [sem("rstd_ready"), sem("scan_rstd_ready")]
        lnT_ps = sem("lnT_ps")
        xT_ready = sem("xT_ready")
        proj_done = sem("proj_done")
        rot_step = sem("rot_step")
        qk_ready = sem("qk_ready")
        v_ps = sem("v_ps")
        v_ready = sem("v_ready")
        scores_done = sem("scores_done")
        max_ready = sem("max_ready")
        exp_ready = sem("exp_ready")
        norm_step = sem("norm_step")
        pT_done = sem("pT_done")
        pd_ready = sem("pd_ready")
        av_done = sem("av_done")
        heads_ready = sem("heads_ready")

        xres_in = sem("xres_in")
        headc_ready = sem("headc_ready")
        filled = [sem("side0_filled"), sem("side1_filled")]
        emptied = [sem("side0_emptied"), sem("side1_emptied")]
        keep1_ready = sem("keep1_ready")
        keep_ready = sem("keep_ready")
        xh_ready = sem("xh_ready")
        xl_ready = sem("xl_ready")
        route_step = sem("route_step")
        gexp_ready = sem("gexp_ready")
        hid_done = sem("hid_done")
        gateb_done = sem("gateb_done")
        silu_ready = sem("silu_ready")
        gated_ready = sem("gated_ready")
        used = sem("used")
        y_done = sem("y_done")
        yT_ready = sem("yT_ready")
        u_ready = sem("u_ready")
        st_ready = sem("st_ready")
        st_zero = sem("st_zero")
        stored = sem("stored")
        ROUTE = 12

        ffn_loads = [(w1raw[:], W1), (w2[:], W2), (b1[:], B1), (b2raw[:], B2), (sb2[:], SB2), (rw[:], RW),
                     (rb[:], RB), (selraw[:], Sel), (acol[:], Acol), (bwT[:], BwT), (bb[:], Bb),
                     (ck[:], Ck), (cd[:], CD), (dwT[:], DwT)]
        ALL_FFN = 16 * len(ffn_loads)

        x_by_batch = X.rearrange("b (k p) d -> b p k d", p=P)
        x_by_chunk = X.rearrange("(k g) (c t) d -> c g t k d", g=2, t=TC)
        out_by_chunk = out.rearrange("(k g) (c t) d -> c g t k d", g=2, t=TC)

        def iterations(eng, body):
            for c in range(-1, STEADY[0]):
                body(c)
            with eng.Fori(*STEADY) as c:
                body(c)
            for c in range(STEADY[1], NC + 3):
                body(c)

        AT = {
            ("finish2", "evacuate"): 3, ("finish2", "transpose"): 5, ("finish2", "add"): 6,
            ("finish1", "evacuate"): 23, ("finish1", "transpose"): 25, ("finish1", "add"): 25,
            ("prepare2", "stats"): 1, ("prepare2", "aggregate"): 2, ("prepare2", "apply0"): 4,
            ("prepare2", "apply2"): 5, ("prepare2", "transpose"): 7, ("prepare2", "keep"): 8,
            ("prepare2", "logits"): 9, ("prepare2", "replace"): 10, ("prepare2", "below_max"): 11,
            ("prepare2", "low"): 12, ("prepare2", "tanh"): 12, ("prepare2", "reciprocal"): 13,
            ("prepare2", "choose"): 14, ("prepare2", "scale"): 15, ("prepare2", "split"): 16,
            ("prepare2", "gateT"): 18,
            ("prepare1", "heads"): 14, ("prepare1", "heads_transpose"): 16, ("prepare1", "x"): 17,
            ("prepare1", "stats"): 18, ("prepare1", "aggregate"): 19, ("prepare1", "apply0"): 21,
            ("prepare1", "apply2"): 22, ("prepare1", "transpose"): 26, ("prepare1", "keep"): 26,
            ("prepare1", "logits"): 28, ("prepare1", "replace"): 29, ("prepare1", "below_max"): 30,
            ("prepare1", "low"): 31, ("prepare1", "tanh"): 31, ("prepare1", "reciprocal"): 32,
            ("prepare1", "choose"): 33, ("prepare1", "scale"): 34, ("prepare1", "split"): 35,
            ("prepare1", "gateT"): 37,
            ("scan_out", "product"): 33, ("scan_out", "add"): 34,
            ("scan_in", "stats"): 27, ("scan_in", "aggregate"): 29, ("scan_in", "apply0"): 30,
            ("scan_in", "apply2"): 31, ("scan_in", "transpose"): 34, ("scan_in", "bu"): 36,
            ("scan_in", "direct"): 38,
        }

        def first_slot(c):
            return (0 <= c < NC) if isinstance(c, int) else True

        def second_slot(c):
            return (2 <= c < NC + 2) if isinstance(c, int) else True

        def scans(c):
            return (1 <= c <= NC) if isinstance(c, int) else True

        def slots(c, main, step, stages):
            for half in (0, 1):
                real = (first_slot, second_slot)[half](c)
                for j in range(NH):
                    at = half * NH + j
                    t = at * STEPS_PER_SLOT
                    if scans(c) and t < TC and step:
                        step(c, t)
                    if real and main:
                        main(half, c, j)
                    for s in range(t + 1, t + STEPS_PER_SLOT):
                        if scans(c) and s < TC and step:
                            step(c, s)
                    stages(half, c, j)

        def stage(half, c, j, task, what):
            return has(task, c) and half * NH + j == AT[task, what]

        block = ctx.enter_context(nc.Block())

        def wait_apart(eng, semaphore, count):
            if not isinstance(count, int):
                count = eng.to_reg(count)
            eng.wait_ge(consts_ready, 1)
            eng.wait_ge(semaphore, count)

        @block.sync
        def _(sp):
            def load_x(b):
                sp.dma_start(xin[:], x_by_batch[bass.ds(b, 1)].rearrange("o p k d -> (o p) k d")).then_inc(x_in, 16)

            load_x(0)
            sp.dma_start(idn[:], ident).then_inc(w_ident, 16)
            sp.dma_start(wqk[:], Wqk).then_inc(w_proj, 16)
            sp.dma_start(wv[:], Wv).then_inc(w_proj, 16)
            sp.wait_ge(ln_step[0], 4)
            load_x(1)
            for dst, src in ffn_loads:
                sp.dma_start(dst, src).then_inc(w_ffn, 16)
            with sp.Fori(2, NB) as b:
                sp.wait_ge(ln_step[0], 4 * b)
                load_x(b)

            def body(c):
                if has("finish2", c):
                    sp.wait_ge(emptied[0], fills(0, "finish2", "y", c) + 1)
                    for g in range(2):
                        dst = out_by_chunk[bass.ds(c - 3, 1), g].rearrange("o t k d -> (o t) k d")
                        sp.dma_start(dst, fin[g * TC:(g + 1) * TC]).then_inc(stored, 16)
                if has("prepare1", c):
                    if not isinstance(c, int) or c >= 0:
                        sp.wait_ge(emptied[1], fills(1, "prepare1", "heads", c - 1) + 1)
                    for g in range(2):
                        src = x_by_chunk[bass.ds(c + 1, 1), g].rearrange("o t k d -> (o t) k d")
                        sp.dma_start(xres[g * TC:(g + 1) * TC], src).then_inc(xres_in, 16)

            iterations(sp, body)
            sp.wait_ge(stored, 32 * NC)

        @block.gpsimd
        def _(pool):
            nc.gpsimd.memset(mhalf[:], -0.5)
            nc.gpsimd.memset(ones2[:], 1.0)
            nc.gpsimd.memset(st[:, :, TC - 1], 0.0).then_inc(consts_ready, 1)

            def inv_std(n, i=0):
                pool.wait_ge(ln_step[i], 4 * n + 3)
                nc.gpsimd.tensor_tensor(rstd[i][:], veps[i][:], mhalf[:], ALU.pow).then_inc(rstd_ready[i], 1)

            def rotated(b):
                for i, dst in enumerate((qT, kT)):
                    if not isinstance(b, int) or b > 0:
                        pool.wait_ge(scores_done, 4 * b)
                    pool.wait_ge(rot_step, 4 * b + 2 * i + 2)
                    nc.gpsimd.tensor_tensor(dst[:], rot[:, 2 * i], rot[:, 2 * i + 1], ALU.add).then_inc(qk_ready, 1)

            pool.wait_ge(consts_ready, 1)
            inv_std(0)
            rotated(0)
            inv_std(1)
            rotated(1)
            inv_std(2)
            with pool.Fori(1, NB - 2) as b:
                rotated(b + 1)
                inv_std(b + 2)
            rotated(NB - 1)
            pool.wait_ge(w_ffn, ALL_FFN)
            nc.gpsimd.tensor_scalar(w1h[:], w1raw[:], 1.0, 0.0, ALU.mult, ALU.add)
            nc.gpsimd.tensor_scalar(b2h[:], b2raw[:], 1.0, 0.0, ALU.mult, ALU.add)
            nc.gpsimd.tensor_scalar(sel[:], selraw[:], 1.0, 0.0, ALU.mult, ALU.add).then_inc(split_hi, 1)

            def stages(half, c, j):
                for i, task in enumerate(("prepare1", "prepare2")):
                    if stage(half, c, j, task, "aggregate"):
                        inv_std(norms(task, c))
                    if stage(half, c, j, task, "logits"):
                        wait_apart(pool, emptied[0], fills(0, task, "x", c) + 1)
                        nc.gpsimd.tensor_scalar(xh[i][:], xT[:], 1.0, 0.0, ALU.mult, ALU.add).then_inc(xh_ready, 1)
                if stage(half, c, j, "scan_in", "aggregate"):
                    inv_std(norms("scan_in", c), 1)

            iterations(pool, lambda c: slots(c, None, None, stages))

        @block.scalar
        def _(act):
            def attend_exp(b, i):
                act.wait_ge(max_ready, 4 * b + i + 1)
                if i >= 2 or not isinstance(b, int) or b > 0:
                    act.wait_ge(pT_done, 4 * b + i - 1)
                nc.scalar.activation(p[:, i % 2], scores_ps[i % 2][:], ACT.Exp, bias=nmax[:, i:i + 1],
                                     accum_out=rsum[:, i:i + 1]).then_inc(exp_ready, 1)

            def copy_xT(b):
                act.wait_ge(lnT_ps, b + 1)
                nc.scalar.copy(xT[:], side_ps[:]).then_inc(xT_ready, 1)

            def copy_v(b):
                act.wait_ge(v_ps, b + 1)
                nc.scalar.copy(v[:].rearrange("p k d -> p (k d)"), side_ps[:]).then_inc(v_ready, 1)

            def copy_heads(b):
                act.wait_ge(av_done, b + 1)
                dst = heads[:, bass.ds(b, 1)].rearrange("p o t -> p (o t)")
                nc.scalar.copy(dst, heads_ps[:]).then_inc(heads_ready, 1)

            act.dma_start(rope[:], ropes).then_inc(w_rope, 16)
            act.dma_start(dtab[:], Dtab).then_inc(w_decay, 16)
            copy_xT(0)
            copy_v(0)

            def attention(b, more):
                attend_exp(b, 0)
                if more:
                    copy_xT(b + 1)
                for i in range(1, 4):
                    attend_exp(b, i)
                copy_heads(b)
                if more:
                    copy_v(b + 1)

            attention(0, True)
            with act.Fori(1, NB - 1) as b:
                attention(b, True)
            attention(NB - 1, False)
            act.wait_ge(w_ffn, ALL_FFN)
            nc.scalar.activation(aexp[:], acol[:], ACT.Exp).then_inc(aexp_ready, 1)

            def main(half, c, j):
                n = job(half, c) * NH + j
                act.wait_ge(hid_done, n + 1)
                if not isinstance(n, int) or n >= NSB:
                    act.wait_ge(used, n - NSB + 1)
                nc.scalar.activation(hid[:, j % NSB], hid_ps[j % 2][:], ACT.Silu, bias=b1[:, j:j + 1]).then_inc(silu_ready, 1)

            def step(c, t):
                act.wait_ge(u_ready, (c - 1) * TC + t + 1)
                nc.scalar.activation(st[:, :, t], u[:], ACT.Tanh).then_inc(st_ready, 1)

            def stages(half, c, j):
                for i, task in enumerate(("finish1", "finish2")):
                    if stage(half, c, j, task, "evacuate"):
                        act.wait_ge(y_done, (job(0, c) if i == 0 else job(1, c - 1)) + 1)
                        nc.scalar.activation(yT[:], y_ps[i][:], ACT.Identity, bias=sb2sum[:]).then_inc(yT_ready, 1)
                if stage(half, c, j, "prepare1", "heads"):
                    if isinstance(c, int) and c < 0:
                        act.wait_ge(heads_ready, NB)
                    else:
                        act.wait_ge(filled[1], fills(1, "prepare1", "heads", c - 1) + 1)
                    src = heads[:, :, bass.ds((c + 1) * TC, TC)]
                    nc.scalar.copy(headc[:], src).then_inc(headc_ready, 1)
                for i, task in enumerate(("prepare1", "prepare2")):
                    if stage(half, c, j, task, "transpose"):
                        act.wait_ge(filled[0], fills(0, task, "x", c) + 1)
                        nc.scalar.copy(xT[:], side[0][:]).then_inc(emptied[0], 1)
                    if stage(half, c, j, task, "tanh"):
                        act.wait_ge(route_step, job(i, c + 1 - i) * ROUTE + 3)
                        nc.scalar.activation(th[:], lg[:, 0], ACT.Tanh, scale=0.5).then_inc(gexp_ready, 1)
                    if stage(half, c, j, task, "gateT"):
                        act.wait_ge(filled[0], fills(0, task, "gate", c) + 1)
                        nc.scalar.copy(gateT[i][:], side[0][:]).then_inc(emptied[0], 1)
                if stage(half, c, j, "scan_in", "transpose"):
                    act.wait_ge(filled[0], fills(0, "scan_in", "x", c) + 1)
                    nc.scalar.copy(xTs[:], side[0][:]).then_inc(emptied[0], 1)

            iterations(act, lambda c: slots(c, main, step, stages))

        @block.vector
        def _(dve):
            def ln_stats(n, x, i=0):
                for k in range(4):
                    last = nc.vector.bn_stats(stats[i][:, k], x[:, k])
                last.then_inc(ln_step[i], 1)

            def ln_aggregate(n, i=0):
                wait_apart(dve, ln_step[i], 4 * n + 1)
                for k in range(4):
                    last = nc.vector.bn_aggr(mv[i][:, k], stats[i][:, k])
                last.then_inc(ln_step[i], 1)
                dve.wait_ge(ln_step[i], 4 * n + 2)
                nc.vector.tensor_scalar(veps[i][:], mv[i][:, :, 1], EPS, None, ALU.add).then_inc(ln_step[i], 1)

            def ln_apply(n, x, y, blocks, i=0):
                dve.wait_ge(rstd_ready[i], n + 1)
                for k in blocks:
                    last = nc.vector.tensor_scalar(y[:, k], x[:, k], mv[i][:, k, 0:1], rstd[i][:, k:k + 1],
                                                   ALU.subtract, ALU.mult)
                if 3 in blocks:
                    last.then_inc(ln_step[i], 1)

            def rotate(b, i):
                dve.wait_ge(proj_done, 2 * b + i + 1)
                if not isinstance(b, int) or b > 0:
                    dve.wait_ge(qk_ready, 2 * b + i - 1)
                for h in range(2):
                    nc.vector.tensor_tensor(rot[:, 2 * i + h], proj_ps[h][:], rope[:, 2 * i + h], ALU.mult).then_inc(rot_step, 1)

            def neg_max(b, i):
                dve.wait_ge(scores_done, 4 * b + i + 1)
                nc.vector.tensor_reduce(nmax[:, i:i + 1], scores_ps[i % 2][:], AX_X, ALU.max, negate=True).then_inc(max_ready, 1)

            def normalise(b, i):
                dve.wait_ge(exp_ready, 4 * b + i + 1)
                nc.vector.reciprocal(rinv[:, i:i + 1], rsum[:, i:i + 1]).then_inc(norm_step, 1)
                dve.wait_ge(norm_step, 8 * b + 2 * i + 1)
                nc.vector.tensor_scalar(p[:, i % 2], p[:, i % 2], rinv[:, i:i + 1], None, ALU.mult).then_inc(norm_step, 1)

            def decay(b, i):
                dve.wait_ge(pT_done, 4 * b + i + 1)
                if i == 0 and (not isinstance(b, int) or b > 0):
                    dve.wait_ge(av_done, b)
                decays = dtab[:, i * P:i * P + 4 * P]
                nc.vector.tensor_tensor(pd[:, :, i * P:(i + 1) * P], pT_ps[i % 2][:].rearrange("p (k q) -> p k q", k=4),
                                        decays.rearrange("p (k q) -> p k q", k=4), ALU.mult).then_inc(pd_ready, 1)

            def layernorm(b):
                dve.wait_ge(x_in, 16 * (b + 1))
                ln_stats(b, xin)
                ln_aggregate(b)
                if not isinstance(b, int) or b > 0:
                    dve.wait_ge(xT_ready, b)
                ln_apply(b, xin, xn, range(4))

            def attention(b, more, still_more):
                neg_max(b, 0)
                neg_max(b, 1)
                normalise(b, 0)
                neg_max(b, 2)
                normalise(b, 1)
                neg_max(b, 3)
                decay(b, 0)
                normalise(b, 2)
                if more:
                    rotate(b + 1, 0)
                decay(b, 1)
                normalise(b, 3)
                decay(b, 2)
                if more:
                    rotate(b + 1, 1)
                decay(b, 3)
                if still_more:
                    layernorm(b + 2)

            layernorm(0)
            dve.wait_ge(w_rope, 16)
            rotate(0, 0)
            rotate(0, 1)
            layernorm(1)
            dve.wait_ge(w_decay, 16)
            attention(0, True, True)
            with dve.Fori(1, NB - 2) as b:
                attention(b, True, True)
            attention(NB - 2, True, False)
            attention(NB - 1, False, False)
            dve.wait_ge(split_hi, 1)
            nc.vector.tensor_tensor(w1l[:], w1raw[:], w1h[:].bitcast(F32), ALU.subtract)
            nc.vector.tensor_tensor(b2l[:], b2raw[:], b2h[:].bitcast(F32), ALU.subtract)
            nc.vector.tensor_tensor(sb2sum[:], sb2[:, 0:1], sb2[:, 1:2], ALU.add).then_inc(split_done, 1)
            dve.wait_ge(aexp_ready, 1)

            def gate_hidden(half, c, j):
                if j < NS:
                    return
                n = job(half, c) * NH + j
                r = job(half, c) * NR + j - NS
                dve.wait_ge(silu_ready, n + 1)
                dve.wait_ge(gateb_done, r + 1)
                nc.vector.tensor_tensor(hid[:, j % NSB], gate_ps[j % 2][:], hid[:, j % NSB], ALU.mult).then_inc(gated_ready, 1)

            def main(half, c, j):
                if j > 0:
                    gate_hidden(half, c, j - 1)

            def step(c, t):
                s = (c - 1) * TC + t
                if t == 0:
                    dve.wait_ge(emptied[1], fills(1, "scan_in", "bu", c - 1) + 1)
                if not isinstance(s, int) or s > 0:
                    dve.wait_ge(st_ready, s)
                nc.vector.scalar_tensor_tensor(u[:], st[:, :, (t - 1) % TC], aexp[:], bu[:, :, t],
                                               ALU.mult, ALU.add).then_inc(u_ready, 1)

            def flat(x):
                return x[:].rearrange("p k d -> p (k d)")

            def spread(cols, n):
                return cols.broadcast_to([P, G, n])

            def stages(half, c, j):
                before_c = c if half else c - 1
                if (first_slot if half else second_slot)(before_c) and j == 0:
                    gate_hidden(1 - half, before_c, NH - 1)
                for i, task in enumerate(("finish1", "finish2")):
                    if stage(half, c, j, task, "add"):
                        dve.wait_ge(filled[0], fills(0, task, "y", c) + 1)
                        if i == 0:
                            dve.wait_ge(keep1_ready, c + 1)
                            nc.vector.tensor_tensor(flat(x2), side[0][:], flat(x1keep), ALU.add).then_inc(emptied[0], 1)
                        else:
                            if not isinstance(c, int) or c > 3:
                                dve.wait_ge(stored, 32 * (c - 3))
                            dve.wait_ge(keep_ready, c - 2)
                            nc.vector.tensor_tensor(flat(fin), side[0][:], flat(x3keep), ALU.add).then_inc(emptied[0], 1)
                if stage(half, c, j, "prepare1", "keep"):
                    if has("finish1", c):
                        dve.wait_ge(emptied[0], fills(0, "finish1", "y", c) + 1)
                    nc.vector.tensor_copy(flat(x1keep), flat(x1)).then_inc(keep1_ready, 1)
                if stage(half, c, j, "prepare2", "keep"):
                    if has("finish2", c):
                        dve.wait_ge(emptied[0], fills(0, "finish2", "y", c) + 1)
                    nc.vector.tensor_copy(flat(x3keep), flat(x3)).then_inc(keep_ready, 1)
                for i, task in enumerate(("prepare1", "prepare2")):
                    x = (x1, x3)[i]
                    if i == 0 and stage(half, c, j, task, "x"):
                        dve.wait_ge(filled[1], fills(1, task, "heads", c) + 1)
                        dve.wait_ge(xres_in, 32 * (c + 2))
                        nc.vector.tensor_tensor(flat(x1), side[1][:], flat(xres), ALU.add).then_inc(emptied[1], 1)
                    if stage(half, c, j, task, "stats"):
                        if i == 0:
                            dve.wait_ge(emptied[1], fills(1, task, "heads", c) + 1)
                        else:
                            dve.wait_ge(emptied[1], fills(1, "scan_out", "y", c - 1) + 1)
                        ln_stats(norms(task, c), x)
                    if stage(half, c, j, task, "aggregate"):
                        ln_aggregate(norms(task, c))
                    for k in (0, 2):
                        if stage(half, c, j, task, f"apply{k}"):
                            ln_apply(norms(task, c), x, xn, (k, k + 1))
                    q = job(i, c + 1 - i)
                    r = q * ROUTE
                    if stage(half, c, j, task, "logits"):
                        u = fills(1, task, "logits", c)
                        dve.wait_ge(filled[1], u + 1)
                        nc.vector.tensor_tensor(lg[:, 0], side[1][:, 0:G * NE].rearrange("p (k e) -> p k e", k=G),
                                                rb[:].rearrange("p (o e) -> p o e", o=1).broadcast_to([P, G, NE]),
                                                ALU.add).then_inc(emptied[1], 1)
                        wait_apart(dve, emptied[1], u + 1)
                        for k in range(G):
                            last = nc.vector.max(top[:, k], lg[:, 0, k])
                        last.then_inc(route_step, 1)
                    if stage(half, c, j, task, "replace"):
                        wait_apart(dve, route_step, r + 1)
                        for k in range(G):
                            last = nc.vector.match_replace(lg[:, 1, k], top[:, k], lg[:, 0, k], LOWEST)
                        last.then_inc(route_step, 1)
                    if stage(half, c, j, task, "below_max"):
                        dve.wait_ge(route_step, r + 2)
                        nc.vector.tensor_tensor(lg[:, 0], lg[:, 0], spread(top[:, :, 0:1], NE), ALU.subtract).then_inc(route_step, 1)
                    if stage(half, c, j, task, "low"):
                        dve.wait_ge(xh_ready, q + 1)
                        nc.vector.tensor_tensor(xl[i][:], xT[:], xh[i][:].bitcast(F32), ALU.subtract).then_inc(xl_ready, 1)
                    if stage(half, c, j, task, "reciprocal"):
                        dve.wait_ge(gexp_ready, q + 1)
                        nc.vector.tensor_scalar(den[:], th[:], -1.0, 1.0, ALU.mult, ALU.add).then_inc(route_step, 1)
                        dve.wait_ge(route_step, r + 4)
                        nc.vector.reciprocal(den[:], den[:]).then_inc(route_step, 1)
                    if stage(half, c, j, task, "choose"):
                        dve.wait_ge(route_step, r + 5)
                        nc.vector.scalar_tensor_tensor(gate[:], th[:], 1.0, den[:], ALU.add, ALU.mult).then_inc(route_step, 1)
                        dve.wait_ge(route_step, r + 6)
                        nc.vector.scalar_tensor_tensor(gate[:], lg[:, 1], LOWEST, gate[:], ALU.is_le, ALU.mult).then_inc(route_step, 1)
                    if stage(half, c, j, task, "scale"):
                        dve.wait_ge(route_step, r + 7)
                        nc.vector.tensor_reduce(gsum[:], gate[:], AX_X, ALU.add).then_inc(route_step, 1)
                        dve.wait_ge(route_step, r + 8)
                        nc.vector.reciprocal(ginv[:], gsum[:]).then_inc(route_step, 1)
                        dve.wait_ge(route_step, r + 9)
                        nc.vector.tensor_tensor(gate[:], gate[:], spread(ginv[:].rearrange("p (k o) -> p k o", o=1), NE), ALU.mult).then_inc(route_step, 1)
                    if stage(half, c, j, task, "split"):
                        dve.wait_ge(route_step, r + 10)
                        nc.vector.tensor_copy(gate2[:, :, 0].bitcast(F32R), gate[:]).then_inc(route_step, 1)
                        dve.wait_ge(route_step, r + 11)
                        nc.vector.tensor_tensor(gate2[:, :, 1].bitcast(F32R), gate[:], gate2[:, :, 0], ALU.subtract).then_inc(route_step, 1)
                if stage(half, c, j, "scan_out", "add"):
                    dve.wait_ge(filled[1], fills(1, "scan_out", "y", c) + 1)
                    nc.vector.tensor_tensor(flat(x3), side[1][:], flat(x2d), ALU.add).then_inc(emptied[1], 1)
                if stage(half, c, j, "scan_in", "stats"):
                    dve.wait_ge(emptied[0], fills(0, "finish1", "y", c) + 1)
                    ln_stats(norms("scan_in", c), x2, 1)
                if stage(half, c, j, "scan_in", "aggregate"):
                    ln_aggregate(norms("scan_in", c), 1)
                for k in (0, 2):
                    if stage(half, c, j, "scan_in", f"apply{k}"):
                        ln_apply(norms("scan_in", c), x2, xns, (k, k + 1), 1)
                if stage(half, c, j, "scan_in", "bu"):
                    dve.wait_ge(filled[1], fills(1, "scan_in", "bu", c) + 1)
                    nc.vector.tensor_scalar(bu[:].rearrange("p g t -> p (g t)"), side[1][:, 0:2 * TC], bb[:], None,
                                            ALU.add).then_inc(emptied[1], 1)
                if stage(half, c, j, "scan_in", "direct"):
                    dve.wait_ge(filled[1], fills(1, "scan_in", "direct", c) + 1)
                    nc.vector.tensor_tensor(flat(x2d), side[1][:], flat(x2), ALU.add).then_inc(emptied[1], 1)

            iterations(dve, lambda c: slots(c, main, step, stages))

        @block.tensor
        def _(pe):
            def transpose4(dst, parts):
                for k in range(4):
                    last = nc.tensor.transpose(dst[:, k * P:(k + 1) * P], parts(k), idn[:])
                return last

            def transposed_x(b):
                pe.wait_ge(ln_step[0], 4 * b + 4)
                if not isinstance(b, int) or b > 0:
                    pe.wait_ge(v_ready, b)
                transpose4(side_ps, lambda k: xn[:, k]).then_inc(lnT_ps, 1)

            def project(b, i):
                if i == 0:
                    pe.wait_ge(xT_ready, b + 1)
                if not isinstance(b, int) or b > 0 or i > 0:
                    pe.wait_ge(rot_step, 4 * b + 2 * i)
                for h in range(2):
                    last = nc.tensor.matmul(proj_ps[h][:], wqk[:, 2 * i + h], xT[:], start=True, stop=True)
                last.then_inc(proj_done, 1)

            def values(b):
                pe.wait_ge(xT_ready, b + 1)
                for k in range(4):
                    last = nc.tensor.matmul(side_ps[:, k * P:(k + 1) * P], xT[:, k * P:(k + 1) * P], wv[:],
                                            start=True, stop=True)
                last.then_inc(v_ps, 1)

            def score(b, i):
                if i == 0:
                    pe.wait_ge(qk_ready, 2 * b + 2)
                if i >= 2:
                    pe.wait_ge(exp_ready, 4 * b + i - 1)
                nc.tensor.matmul(scores_ps[i % 2][:], qT[:, i * P:(i + 1) * P], kT[:], start=True, stop=True).then_inc(scores_done, 1)

            def weights(b, i):
                pe.wait_ge(norm_step, 8 * b + 2 * i + 2)
                if i >= 2:
                    pe.wait_ge(pd_ready, 4 * b + i - 1)
                transpose4(pT_ps[i % 2], lambda k: p[:, i % 2, (3 - k) * P:(4 - k) * P]).then_inc(pT_done, 1)

            def attend(b):
                pe.wait_ge(pd_ready, 4 * b + 4)
                pe.wait_ge(v_ready, b + 1)
                if not isinstance(b, int) or b > 0:
                    pe.wait_ge(heads_ready, b)
                for k in range(4):
                    last = nc.tensor.matmul(heads_ps[:], v[:, 3 - k], pd[:, k], start=(k == 0), stop=(k == 3))
                last.then_inc(av_done, 1)

            def attention(b, more):
                score(b, 0)
                score(b, 1)
                if more:
                    transposed_x(b + 1)
                score(b, 2)
                if more:
                    project(b + 1, 0)
                score(b, 3)
                weights(b, 0)
                weights(b, 1)
                if more:
                    project(b + 1, 1)
                weights(b, 2)
                weights(b, 3)
                attend(b)
                if more:
                    values(b + 1)

            pe.wait_ge(w_ident, 16)
            transposed_x(0)
            pe.wait_ge(w_proj, 32)
            project(0, 0)
            project(0, 1)
            values(0)
            attention(0, True)
            with pe.Fori(1, NB - 1) as b:
                attention(b, True)
            attention(NB - 1, False)
            pe.wait_ge(split_done, 1)
            pe.wait_ge(consts_ready, 1)

            def second_product(half, c, j):
                q = job(half, c)
                if j < NS:
                    pe.wait_ge(silu_ready, q * NH + j + 1)
                else:
                    pe.wait_ge(gated_ready, q * NR + j - NS + 1)
                nc.tensor.matmul(y_ps[half][:], w2[:, j], hid[:, j % NSB], start=(j == 0), stop=False).then_inc(used, 1)
                if j == NH - 1:
                    nc.tensor.matmul(y_ps[half][:], b2l[:], gateT[half][:], start=False, stop=False)
                    nc.tensor.matmul(y_ps[half][:], b2h[:], gateT[half][:], start=False, stop=True).then_inc(y_done, 1)

            def main(half, c, j):
                q = job(half, c)
                n = q * NH + j
                r = q * NR + j - NS
                if j == 0:
                    pe.wait_ge(xl_ready, q + 1)
                if not isinstance(n, int) or n >= 2:
                    pe.wait_ge(silu_ready, n - 1)
                cols = slice(j * P, (j + 1) * P)
                nc.tensor.matmul(hid_ps[j % 2][:], w1l[:, cols], xh[half][:], start=True, stop=False)
                nc.tensor.matmul(hid_ps[j % 2][:], w1h[:, cols], xl[half][:], start=False, stop=False)
                nc.tensor.matmul(hid_ps[j % 2][:], w1h[:, cols], xh[half][:], start=False, stop=True).then_inc(hid_done, 1)
                if j >= NS:
                    if j == NS:
                        task, at = (("prepare1", c - 1), ("prepare2", c))[half]
                        pe.wait_ge(emptied[0], fills(0, task, "gate", at) + 1)
                    if not isinstance(r, int) or r >= 2:
                        pe.wait_ge(gated_ready, r - 1)
                    g = j - NS
                    nc.tensor.matmul(gate_ps[j % 2][:], sel[:, g * P:(g + 1) * P], gateT[half][:],
                                     start=True, stop=True).then_inc(gateb_done, 1)
                if j >= LAG:
                    second_product(half, c, j - LAG)

            def fill(bank, task, what, c):
                n = fills(bank, task, what, c)
                if not isinstance(n, int) or n > 0:
                    pe.wait_ge(emptied[bank], n)

            def stages(half, c, j):
                before_c = c if half else c - 1
                if (first_slot if half else second_slot)(before_c) and j < LAG:
                    second_product(1 - half, before_c, NH - LAG + j)
                for i, task in enumerate(("finish1", "finish2")):
                    if stage(half, c, j, task, "transpose"):
                        pe.wait_ge(yT_ready, (job(0, c) if i == 0 else job(1, c - 1)) + 1)
                        fill(0, task, "y", c)
                        transpose4(side[0], lambda k: yT[:, k * P:(k + 1) * P]).then_inc(filled[0], 1)
                if stage(half, c, j, "prepare1", "heads_transpose"):
                    pe.wait_ge(headc_ready, c + 2)
                    fill(1, "prepare1", "heads", c)
                    transpose4(side[1], lambda k: headc[:, 2 * k:2 * k + 2].rearrange("p g t -> p (g t)")).then_inc(filled[1], 1)
                for i, task in enumerate(("prepare1", "prepare2")):
                    if stage(half, c, j, task, "transpose"):
                        pe.wait_ge(ln_step[0], 4 * norms(task, c) + 4)
                        fill(0, task, "x", c)
                        transpose4(side[0], lambda k: xn[:, k]).then_inc(filled[0], 1)
                    if stage(half, c, j, task, "logits"):
                        pe.wait_ge(emptied[0], fills(0, task, "x", c) + 1)
                        fill(1, task, "logits", c)
                        for k in range(G):
                            last = nc.tensor.matmul(side[1][:, k * NE:(k + 1) * NE], xT[:, k * P:(k + 1) * P], rw[:],
                                                    start=True, stop=True)
                        last.then_inc(filled[1], 1)
                    if stage(half, c, j, task, "gateT"):
                        pe.wait_ge(route_step, (job(i, c + 1 - i) + 1) * ROUTE)
                        fill(0, task, "gate", c)
                        transpose4(side[0], lambda k: gate2[:, k].rearrange("p h e -> p (h e)")).then_inc(filled[0], 1)
                if stage(half, c, j, "scan_out", "product"):
                    pe.wait_ge(st_ready, c * TC)
                    fill(1, "scan_out", "y", c)
                    for k in range(G):
                        last = nc.tensor.matmul(side[1][:, k * P:(k + 1) * P], st[:].rearrange("p g t -> p (g t)"),
                                                ck[:, k], start=True, stop=True)
                    last.then_inc(filled[1], 1)
                if stage(half, c, j, "scan_in", "transpose"):
                    pe.wait_ge(ln_step[1], 4 * norms("scan_in", c) + 4)
                    fill(0, "scan_in", "x", c)
                    transpose4(side[0], lambda k: xns[:, k]).then_inc(filled[0], 1)
                if stage(half, c, j, "scan_in", "bu"):
                    pe.wait_ge(emptied[0], fills(0, "scan_in", "x", c) + 1)
                    fill(1, "scan_in", "bu", c)
                    for k in range(G):
                        last = nc.tensor.matmul(side[1][k * STATE:(k + 1) * STATE, 0:P], bwT[:], xTs[:, k * P:(k + 1) * P],
                                                start=True, stop=True)
                    last.then_inc(filled[1], 1)
                if stage(half, c, j, "scan_in", "direct"):
                    fill(1, "scan_in", "direct", c)
                    for k in range(G):
                        dst = side[1][:, k * P:(k + 1) * P]
                        nc.tensor.matmul(dst, xTs[:, k * P:(k + 1) * P], dwT[:], start=True, stop=False)
                        last = nc.tensor.matmul(dst, ones2[:], cd[:], start=False, stop=True)
                    last.then_inc(filled[1], 1)

            iterations(pe, lambda c: slots(c, main, None, stages))


def tables():
    half = D // 2
    f = np.float32
    scale_vec = (np.arange(0, D, 2, dtype=f) + f(0.4 * D)) / f(1.4 * D)
    power = np.arange(L, dtype=f) / f(SCALE_BASE)
    scale = (scale_vec[None, :] ** power[:, None]).astype(f)
    inv_freq = (f(1.0) / f(10000.0) ** (np.arange(half, dtype=f) / f(half))).astype(f)
    angle = np.arange(L, dtype=f)[:, None] * inv_freq[None, :]
    sign = np.where(np.arange(D) % 2 == 0, f(-1), f(1))[None, :]
    rows = []
    for s in (scale, f(1.0) / scale):
        rows.append(np.repeat(np.cos(angle) * s, 2, axis=-1).T)
        rows.append((np.repeat(np.sin(angle) * s, 2, axis=-1) * sign).T)
    ropes = np.ascontiguousarray(np.stack(rows, axis=1), dtype=f)
    i = np.arange(3 * P + L)[None, :]
    decay = (GAMMA ** np.abs(i - 3 * P - np.arange(P)[:, None])).astype(f)
    sel = np.zeros((P, NR, P), f)
    for j in range(NR):
        for m in range(P):
            e = j * (P // HE) + m // HE
            sel[e, j, m] = sel[NE + e, j, m] = 1.0
    return ropes, decay, np.eye(P, dtype=f), sel.reshape(P, NR * P)


def kernel(**inputs):
    import concourse.bacc as bacc
    from concourse.bass_utils import run_bass_kernel_spmd

    a = {k.replace("L0_", ""): np.asarray(v) for k, v in inputs.items()}
    swap = np.arange(D) ^ 1
    wq, wk = a["attn_a_W_Q"], a["attn_a_W_K"]
    ropes, decay, eye, sel = tables()
    ck = np.zeros((P, G, D), np.float32)
    for k in range(G):
        ck[k * STATE:(k + 1) * STATE, k] = a["attn_b_C_w"].T
    w1 = np.concatenate([a["ffn_sw1"].transpose(1, 0, 2).reshape(D, NS * P),
                         a["ffn_w1"].transpose(1, 0, 2).reshape(D, NR * P)], axis=1)
    w2 = np.concatenate([a["ffn_sw2"].reshape(NS, P, D), a["ffn_w2"].reshape(NR, P, D)]).transpose(1, 0, 2)
    b1 = np.concatenate([a["ffn_sb1"].reshape(NS, P), a["ffn_b1"].reshape(NR, P)]).T
    arrays = {
        "X": a["attn_a_X"],
        "Wqk": np.stack([wq, wq[:, swap], wk, wk[:, swap]], axis=1),
        "Wv": a["attn_a_W_V"], "ropes": ropes, "Dtab": decay, "ident": eye,
        "W1": w1, "W2": w2, "B1": b1, "B2": np.concatenate([a["ffn_b2"]] * 2), "SB2": a["ffn_sb2"].T,
        "RW": a["ffn_router_w"], "RB": np.tile(a["ffn_router_b"][None], (P, 1)), "Sel": sel,
        "Acol": np.tile(a["attn_b_A"], G)[:, None], "BwT": a["attn_b_B_w"].T,
        "Bb": np.tile(a["attn_b_B_b"], G)[:, None], "Ck": ck,
        "CD": np.stack([a["attn_b_C_b"], a["attn_b_D_b"]]), "DwT": a["attn_b_D_w"].T,
    }
    arrays = {k: np.ascontiguousarray(x) for k, x in arrays.items()}
    nc = bacc.Bacc("TRN2", target_bir_lowering=False, num_devices=1)
    aps = [nc.dram_tensor(k, x.shape, F32, kind="ExternalInput").ap() for k, x in arrays.items()]
    out = nc.dram_tensor("out", (NB, L, D), F32, kind="ExternalOutput").ap()
    program(nc, *aps, out)
    r = run_bass_kernel_spmd(nc, [arrays], core_ids=[0])
    return r.results[0]["out"]
```

```python
from contextlib import ExitStack

import numpy as np
import concourse.bass as bass
from concourse import mybir

F32 = mybir.dt.float32
F32R = mybir.dt.float32r
ALU = mybir.AluOpType
ACT = mybir.ActivationFunctionType
AX_X = mybir.AxisListType.X

P = 128
NB, L, D = 8, 512, 128
NE, HE = 64, 32
TC = 64
NC = L // TC
G = NB // 2
NS = 4
NR = NE * HE // P
NH = NS + NR
STATE = 32
GATE_LAG, HI_LAG, LO_LAG, LAG = 1, 2, 3, 4
NSB = LAG + 1
NPB = 4
SPLIT = (0, 1, 2, 3, 5, 7, 10, 12, 15, 17)
LO_POOL = (1, 5, 7, 10, 12, 15, 17)
LO_DVE = tuple(j for j in SPLIT if j not in LO_POOL)
EPS = 1e-5
GAMMA = 0.9
SCALE_BASE = 512.0
STEPS_PER_SLOT = 2
LAST_STEPS = 18
SPLITS = 5
LOWEST = -3.0e38

SIDE = {
    "gates1": (0, NC - 1),
    "finish2": (3, NC + 2),
    "prepare2": (2, NC + 1),
    "finish1": (0, NC - 1),
    "prepare1": (-1, NC - 2),
    "scan_out": (1, NC),
    "scan_in": (0, NC - 1),
}
STEADY = (3, NC - 1)
FILLS = (
    (("gates1", "gate"), ("finish2", "y"), ("prepare2", "x"), ("prepare2", "gate"), ("finish1", "y"),
     ("prepare1", "x"), ("scan_in", "x")),
    (("prepare2", "logits"), ("prepare1", "heads"), ("prepare1", "logits"), ("scan_out", "y"),
     ("scan_in", "bu"), ("scan_in", "direct")),
)
EARLY = (0, 1)
FILLS_EARLY = ((("gates1", "gate"), ("prepare1", "x"), ("finish1", "y"), ("scan_in", "x")), FILLS[1])


def has(task, c):
    return not isinstance(c, int) or SIDE[task][0] <= c <= SIDE[task][1]


def steps_by(c, slot):
    if isinstance(c, int) and c == NC:
        steps = LAST_STEPS * slot // NH if slot < NH else LAST_STEPS + (TC - LAST_STEPS) * (slot - NH) // NH
    else:
        steps = STEPS_PER_SLOT * slot
    return min(TC, steps)


def before(task, c):
    lo, hi = SIDE[task]
    return max(0, min(c - lo, hi - lo + 1)) if isinstance(c, int) else c - lo


def early(c):
    return isinstance(c, int) and c in EARLY


def fills(bank, task, what, c):
    total = 0
    for name, _ in FILLS[bank]:
        total = total + before(name, c)
    order = (FILLS_EARLY if early(c) else FILLS)[bank]
    return total + sum(1 for name, _ in order[:order.index((task, what))] if has(name, c))


def norms(task, c):
    if task == "scan_in":
        return before(task, c)
    same = 1 if task == "prepare1" and has("prepare2", c) else 0
    return NB + before("prepare1", c) + before("prepare2", c) + same


def job(second, c):
    if not isinstance(c, int):
        return 2 * c - 2 + second
    first_before = max(0, min(c, NC))
    second_before = max(0, min(c - 2, NC))
    return first_before + second_before + (1 if second and 0 <= c < NC else 0)


def nth(chunks, q, j):
    return q * len(chunks) + chunks.index(j) + 1


def program(nc, X, Wqk, Wv, ropes, Dtab, ident, W1, W2, B1, B2, SB2, RW, RB, Sel, Acol, BwT, Bb, Ck,
            CD, DwT, out):
    ctx = ExitStack()
    with ctx:
        def sb(name, shape, dt=F32, within=ctx):
            return within.enter_context(nc.sbuf_tensor(name, shape, dt))

        def sem(name):
            return ctx.enter_context(nc.semaphore(name))

        ps = [ctx.enter_context(nc.psum_tensor(f"bank{i}", [P, 512], F32)) for i in range(8)]
        scores_ps, pT_ps, heads_ps = ps[0:2], ps[2:4], ps[4]
        proj_ps, side_ps = [ps[5], ps[7]], ps[6]
        hid_ps, gate_ps, y_ps, side = ps[0:2], ps[2:4], ps[4:6], ps[6:8]

        idn = sb("idn", [P, P])
        w1h = sb("w1h", [P, NH * P], F32R)
        w1l = sb("w1l", [P, NH * P], F32R)
        w2 = sb("w2", [P, NH * D])
        w2h = sb("w2h", [P, NH * D], F32R)
        w2l = sb("w2l", [P, NH * D], F32R)
        b1 = sb("b1", [P, NH])
        b2raw = sb("b2raw", [P, D])
        b2h = sb("b2h", [P, D], F32R)
        b2l = sb("b2l", [P, D], F32R)
        sb2 = sb("sb2", [P, 2])
        sb2sum = sb("sb2sum", [P, 1])
        rw = sb("rw", [P, NE])
        rb = sb("rb", [P, NE])
        sel = sb("sel", [P, NR * P], F32R)
        acol = sb("acol", [P, 1])
        aexp = sb("aexp", [P, 1])
        bwT = sb("bwT", [P, STATE])
        bb = sb("bb", [P, 1])
        ck = sb("ck", [P, G, D])
        cd = sb("cd", [2, D])
        ones2 = sb("ones2", [2, P])
        dwT = sb("dwT", [P, D])
        mhalf = sb("mhalf", [P, 4])

        stats = [sb(f"stats{i}", [P, 4, 6]) for i in range(2)]
        mv = [sb(f"mv{i}", [P, 4, 2]) for i in range(2)]
        veps = [sb(f"veps{i}", [P, 4]) for i in range(2)]
        rstd = [sb(f"rstd{i}", [P, 4]) for i in range(2)]
        xn = sb("xn", [P, 4, D])
        xT = sb("xT", [P, 512])
        xns = sb("xns", [P, 4, D])
        xTs = sb("xTs", [P, 512])

        heads = sb("heads", [P, NB, L])

        xres = sb("xres", [P, G, D])
        headc = sb("headc", [P, NB, TC])
        x1 = sb("x1", [P, G, D])
        x1keep = sb("x1keep", [P, G, D])
        x2 = sb("x2", [P, G, D])
        x2d = sb("x2d", [P, G, D])
        x3 = sb("x3", [P, G, D])
        x3keep = sb("x3keep", [P, G, D])
        fin = sb("fin", [P, G, D])

        bu = sb("bu", [P, 2, TC])
        st = sb("st", [P, 2, TC])
        u = sb("u", [P, 2])

        attn = ExitStack()
        wqk = sb("wqk", [P, 4, D], within=attn)
        wv = sb("wv", [P, D], within=attn)
        rope = sb("rope", [P, 4, L], within=attn)
        dtab = sb("dtab", [P, 3 * P + L], within=attn)
        xin = sb("xin", [P, 4, D], within=attn)
        rot = sb("rot", [P, 4, L], within=attn)
        qT = sb("qT", [P, L], within=attn)
        kT = sb("kT", [P, L], within=attn)
        v = sb("v", [P, 4, D], within=attn)
        nmax = sb("nmax", [P, 4], within=attn)
        rsum = sb("rsum", [P, 4], within=attn)
        rinv = sb("rinv", [P, 4], within=attn)
        p = sb("p", [P, 4, L], within=attn)
        pd = sb("pd", [P, 4, L], within=attn)
        w1 = sb("w1", [P, NH * P], within=attn)
        selraw = sb("selraw", [P, NR * P], within=attn)
        attn.close()

        xh = [sb(f"xh{i}", [P, 512], F32R) for i in range(2)]
        xl = [sb(f"xl{i}", [P, 512], F32R) for i in range(2)]
        gateT = [sb(f"gateT{i}", [P, 512], F32R) for i in range(2)]
        lg = sb("lg", [P, 2, G, NE])
        top = sb("top", [P, G, 8])
        th = sb("th", [P, G, NE])
        den = sb("den", [P, G, NE])
        gsum = sb("gsum", [P, G])
        ginv = sb("ginv", [P, G])
        gate = sb("gate", [P, G, NE])
        gate2 = sb("gate2", [P, G, 2, NE])
        hid = sb("hid", [P, NSB, 512])
        hid_hi = sb("hid_hi", [P, NPB, 512], F32R)
        hid_lo = sb("hid_lo", [P, NPB, 512], F32R)
        yT = sb("yT", [P, 512])

        w_proj = sem("w_proj")
        w_rope = sem("w_rope")
        w_decay = sem("w_decay")
        w_ident = sem("w_ident")
        w_split = sem("w_split")
        w_ffn = sem("w_ffn")
        consts_ready = sem("consts_ready")
        split_hi = sem("split_hi")
        split_lo = sem("split_lo")
        sel_ready = sem("sel_ready")
        split_b = sem("split_b")
        split_done = sem("split_done")
        aexp_ready = sem("aexp_ready")
        x_in = sem("x_in")
        ln_step = [sem("ln_step"), sem("scan_ln_step")]
        rstd_ready = [sem("rstd_ready"), sem("scan_rstd_ready")]
        lnT_ps = sem("lnT_ps")
        xT_ready = sem("xT_ready")
        proj_done = sem("proj_done")
        rot_step = sem("rot_step")
        qk_ready = sem("qk_ready")
        v_ps = sem("v_ps")
        v_ready = sem("v_ready")
        scores_done = sem("scores_done")
        max_ready = sem("max_ready")
        exp_ready = sem("exp_ready")
        rinv_ready = sem("rinv_ready")
        norm_ready = sem("norm_ready")
        pT_done = sem("pT_done")
        pd_ready = sem("pd_ready")
        av_done = sem("av_done")
        heads_ready = sem("heads_ready")

        xres_in = sem("xres_in")
        headc_ready = sem("headc_ready")
        filled = [sem("side0_filled"), sem("side1_filled")]
        emptied = [sem("side0_emptied"), sem("side1_emptied")]
        keep1_ready = sem("keep1_ready")
        keep_ready = sem("keep_ready")
        xh_ready = sem("xh_ready")
        xl_ready = sem("xl_ready")
        route_step = sem("route_step")
        gexp_ready = sem("gexp_ready")
        hid_done = sem("hid_done")
        gateb_done = sem("gateb_done")
        silu_ready = sem("silu_ready")
        gated_ready = sem("gated_ready")
        hi_ready = sem("hi_ready")
        lo_dve = sem("lo_dve")
        lo_pool = sem("lo_pool")
        used = sem("used")
        y_done = sem("y_done")
        yT_ready = sem("yT_ready")
        u_ready = sem("u_ready")
        st_ready = sem("st_ready")
        st_zero = sem("st_zero")
        stored = sem("stored")
        ROUTE = 12

        ffn_loads = [(b1[:], B1), (b2raw[:], B2), (sb2[:], SB2), (rw[:], RW),
                     (rb[:], RB), (selraw[:], Sel), (acol[:], Acol), (bwT[:], BwT), (bb[:], Bb),
                     (ck[:], Ck), (cd[:], CD), (dwT[:], DwT)]
        ALL_FFN = 16 * len(ffn_loads)

        x_by_batch = X.rearrange("b (k p) d -> b p k d", p=P)
        x_by_chunk = X.rearrange("(k g) (c t) d -> c g t k d", g=2, t=TC)
        out_by_chunk = out.rearrange("(k g) (c t) d -> c g t k d", g=2, t=TC)

        def iterations(eng, body):
            for c in range(-1, STEADY[0]):
                body(c)
            with eng.Fori(*STEADY) as c:
                body(c)
            for c in range(STEADY[1], NC + 3):
                body(c)

        AT = {
            ("finish2", "evacuate"): 5, ("finish2", "transpose"): 7, ("finish2", "add"): 7,
            ("finish1", "evacuate"): 25, ("finish1", "transpose"): 27, ("finish1", "add"): 27,
            ("prepare2", "stats"): 1, ("prepare2", "aggregate"): 2, ("prepare2", "apply0"): 4,
            ("prepare2", "apply2"): 5, ("prepare2", "transpose"): 8, ("prepare2", "keep"): 9,
            ("prepare2", "high"): 10, ("prepare2", "logits"): 10, ("prepare2", "low"): 11,
            ("prepare2", "maxima"): 11, ("prepare2", "replace"): 12, ("prepare2", "below_max"): 12, ("prepare2", "tanh"): 13, ("prepare2", "reciprocal"): 14,
            ("prepare2", "choose"): 15, ("prepare2", "scale"): 16, ("prepare2", "split"): 17,
            ("prepare2", "gateT"): 22,
            ("prepare1", "heads"): 14, ("prepare1", "heads_transpose"): 16, ("prepare1", "x"): 17,
            ("prepare1", "stats"): 18, ("prepare1", "aggregate"): 19, ("prepare1", "apply0"): 21,
            ("prepare1", "apply2"): 22, ("prepare1", "transpose"): 28, ("prepare1", "keep"): 28,
            ("prepare1", "high"): 30, ("prepare1", "logits"): 30, ("prepare1", "low"): 31,
            ("prepare1", "maxima"): 31, ("prepare1", "replace"): 32, ("prepare1", "below_max"): 32, ("prepare1", "tanh"): 33, ("prepare1", "reciprocal"): 34,
            ("prepare1", "choose"): 35, ("prepare1", "scale"): 36, ("prepare1", "split"): 37,
            ("gates1", "gateT"): 2,
            ("scan_out", "product"): 33, ("scan_out", "add"): 34,
            ("scan_in", "stats"): 29, ("scan_in", "aggregate"): 30, ("scan_in", "apply0"): 32,
            ("scan_in", "apply2"): 33, ("scan_in", "transpose"): 35, ("scan_in", "bu"): 37,
            ("scan_in", "direct"): 38, ("scan_in", "add"): 39,
        }

        AT_EARLY = {
            ("prepare1", "heads"): 1, ("prepare1", "heads_transpose"): 2, ("prepare1", "x"): 3,
            ("prepare1", "stats"): 4, ("prepare1", "aggregate"): 5, ("prepare1", "apply0"): 7,
            ("prepare1", "apply2"): 8, ("prepare1", "transpose"): 10, ("prepare1", "logits"): 12,
            ("prepare1", "maxima"): 13, ("prepare1", "replace"): 14, ("prepare1", "below_max"): 14,
            ("prepare1", "tanh"): 15, ("prepare1", "reciprocal"): 16, ("prepare1", "choose"): 17,
            ("prepare1", "scale"): 18, ("prepare1", "split"): 19,
            ("prepare1", "high"): 20, ("prepare1", "low"): 21,
        }
        AT_LAST = {("scan_out", "product"): NH + NH - 1, ("scan_out", "add"): NH + NH - 1}

        def first_slot(c):
            return (0 <= c < NC) if isinstance(c, int) else True

        def second_slot(c):
            return (2 <= c < NC + 2) if isinstance(c, int) else True

        def scans(c):
            return (1 <= c <= NC) if isinstance(c, int) else True

        def weight_group(g):
            return bass.ds(g * (NH * P // SPLITS), NH * P // SPLITS)

        def flat(x):
            return x[:].rearrange("p k d -> p (k d)")

        def behind(half, c, j, lag):
            if j < lag:
                half, c, j = 1 - half, (c if half else c - 1), j + NH
            return [(half, c, j - lag)] if (first_slot, second_slot)[half](c) else []

        def wait_hidden(eng, q, j):
            if j < NS:
                eng.wait_ge(silu_ready, q * NH + j + 1)
            else:
                eng.wait_ge(gated_ready, q * NR + j - NS + 1)

        def slots(c, main, step, stages, late=None):
            for half in (0, 1):
                for j in range(NH):
                    at = half * NH + j
                    steps = range(steps_by(c, at), steps_by(c, at + 1)) if scans(c) and step else ()
                    for t in steps[:1]:
                        step(c, t)
                    if main:
                        main(half, c, j)
                    for t in steps[1:]:
                        step(c, t)
                    if late:
                        late(half, c, j)
                    stages(half, c, j)

        def stage(half, c, j, task, what):
            at = AT[task, what]
            if early(c):
                at = AT_EARLY.get((task, what), at)
            elif isinstance(c, int) and c == NC:
                at = AT_LAST.get((task, what), at)
            return has(task, c) and half * NH + j == at

        block = ctx.enter_context(nc.Block())

        def wait_apart(eng, semaphore, count):
            if not isinstance(count, int):
                count = eng.to_reg(count)
            eng.wait_ge(consts_ready, 1)
            eng.wait_ge(semaphore, count)

        @block.sync
        def _(sp):
            def load_x(b):
                sp.dma_start(xin[:], x_by_batch[bass.ds(b, 1)].rearrange("o p k d -> (o p) k d")).then_inc(x_in, 16)

            load_x(0)
            sp.dma_start(idn[:], ident).then_inc(w_ident, 16)
            sp.dma_start(wqk[:], Wqk).then_inc(w_proj, 16)
            sp.dma_start(wv[:], Wv).then_inc(w_proj, 16)
            sp.wait_ge(ln_step[0], 4)
            load_x(1)
            sp.dma_start(w1[:], W1).then_inc(w_split, 16)
            sp.dma_start(w2[:], W2).then_inc(w_split, 16)
            for dst, src in ffn_loads:
                sp.dma_start(dst, src).then_inc(w_ffn, 16)
            with sp.Fori(2, NB) as b:
                sp.wait_ge(ln_step[0], 4 * b)
                load_x(b)

            def body(c):
                if has("finish2", c):
                    sp.wait_ge(emptied[0], fills(0, "finish2", "y", c) + 1)
                    for g in range(2):
                        dst = out_by_chunk[bass.ds(c - 3, 1), g].rearrange("o t k d -> (o t) k d")
                        sp.dma_start(dst, fin[g * TC:(g + 1) * TC]).then_inc(stored, 16)
                if has("prepare1", c):
                    if not isinstance(c, int) or c >= 0:
                        sp.wait_ge(emptied[1], fills(1, "prepare1", "heads", c - 1) + 1)
                    for g in range(2):
                        src = x_by_chunk[bass.ds(c + 1, 1), g].rearrange("o t k d -> (o t) k d")
                        sp.dma_start(xres[g * TC:(g + 1) * TC], src).then_inc(xres_in, 16)

            iterations(sp, body)
            sp.wait_ge(stored, 32 * NC)

        @block.gpsimd
        def _(pool):
            nc.gpsimd.memset(mhalf[:], -0.5)
            nc.gpsimd.memset(ones2[:], 1.0)
            nc.gpsimd.memset(st[:, :, TC - 1], 0.0).then_inc(consts_ready, 1)

            def inv_std(n, i=0):
                pool.wait_ge(ln_step[i], 4 * n + 3)
                nc.gpsimd.tensor_tensor(rstd[i][:], veps[i][:], mhalf[:], ALU.pow).then_inc(rstd_ready[i], 1)

            def rotated(b, i):
                dst = (qT, kT)[i]
                if not isinstance(b, int) or b > 0:
                    pool.wait_ge(scores_done, 4 * b)
                pool.wait_ge(rot_step, 4 * b + 2 * i + 2)
                nc.gpsimd.tensor_tensor(dst[:], rot[:, 2 * i], rot[:, 2 * i + 1], ALU.add).then_inc(qk_ready, 1)

            pool.wait_ge(consts_ready, 1)
            inv_std(0)
            rotated(0, 0)
            rotated(0, 1)
            inv_std(1)
            rotated(1, 0)
            inv_std(2)
            rotated(1, 1)
            with pool.Fori(0, SPLITS) as g:
                rotated(g + 2, 0)
                inv_std(g + 3)
                rotated(g + 2, 1)
                group = weight_group(g)
                pool.wait_ge(split_hi, g + 1)
                nc.gpsimd.tensor_tensor(w1l[:, group], w1[:, group], w1h[:, group].bitcast(F32), ALU.subtract)
                nc.gpsimd.tensor_tensor(w2l[:, group], w2[:, group], w2h[:, group].bitcast(F32), ALU.subtract).then_inc(split_lo, 1)
            rotated(NB - 1, 0)
            rotated(NB - 1, 1)
            pool.wait_ge(w_ffn, ALL_FFN)
            nc.gpsimd.tensor_scalar(b2h[:], b2raw[:], 1.0, 0.0, ALU.mult, ALU.add).then_inc(split_b, 1)
            nc.gpsimd.tensor_scalar(sel[:], selraw[:], 1.0, 0.0, ALU.mult, ALU.add).then_inc(sel_ready, 1)

            def stages(half, c, j):
                for i, task in enumerate(("prepare1", "prepare2")):
                    if stage(half, c, j, task, "aggregate"):
                        inv_std(norms(task, c))
                    if stage(half, c, j, task, "high"):
                        if i == 0 and early(c):
                            pool.wait_ge(hid_done, (job(0, c) + 1) * NH)
                        wait_apart(pool, emptied[0], fills(0, task, "x", c) + 1)
                        nc.gpsimd.tensor_scalar(xh[i][:], xT[:], 1.0, 0.0, ALU.mult, ALU.add).then_inc(xh_ready, 1)
                if stage(half, c, j, "scan_in", "aggregate"):
                    inv_std(norms("scan_in", c), 1)

            def low_part(half, c, j):
                for half, c, j in behind(half, c, j, HI_LAG):
                    if j in LO_POOL:
                        pool.wait_ge(hi_ready, nth(SPLIT, job(half, c), j))
                        nc.gpsimd.tensor_tensor(hid_lo[:, j % NPB], hid[:, j % NSB], hid_hi[:, j % NPB].bitcast(F32),
                                                ALU.subtract).then_inc(lo_pool, 1)

            iterations(pool, lambda c: slots(c, low_part, None, stages))

        @block.scalar
        def _(act):
            def attend_exp(b, i):
                act.wait_ge(max_ready, 4 * b + i + 1)
                if not isinstance(b, int) or b > 0:
                    act.wait_ge(pT_done, 4 * (b - 1) + i + 1)
                nc.scalar.activation(p[:, i], scores_ps[i % 2][:], ACT.Exp, bias=nmax[:, i:i + 1],
                                     accum_out=rsum[:, i:i + 1]).then_inc(exp_ready, 1)

            def normalise(b, i):
                act.wait_ge(rinv_ready, 4 * b + i + 1)
                nc.scalar.mul(p[:, i], p[:, i], rinv[:, i:i + 1]).then_inc(norm_ready, 1)

            def copy_xT(b):
                act.wait_ge(lnT_ps, b + 1)
                nc.scalar.copy(xT[:], proj_ps[1][:]).then_inc(xT_ready, 1)

            def copy_v(b):
                act.wait_ge(v_ps, b + 1)
                nc.scalar.copy(v[:].rearrange("p k d -> p (k d)"), side_ps[:]).then_inc(v_ready, 1)

            def copy_heads(b):
                act.wait_ge(av_done, b + 1)
                dst = heads[:, bass.ds(b, 1)].rearrange("p o t -> p (o t)")
                nc.scalar.copy(dst, heads_ps[:]).then_inc(heads_ready, 1)

            act.dma_start(rope[:], ropes).then_inc(w_rope, 16)
            act.dma_start(dtab[:], Dtab).then_inc(w_decay, 16)
            copy_xT(0)
            copy_v(0)

            def attention(b, more):
                if more:
                    copy_xT(b + 1)
                for i in (0, 2):
                    attend_exp(b, i)
                    attend_exp(b, i + 1)
                    normalise(b, i)
                    normalise(b, i + 1)
                copy_heads(b)
                if more:
                    copy_v(b + 1)

            attention(0, True)
            act.wait_ge(w_split, 32)
            with act.Fori(1, SPLITS + 1) as b:
                attention(b, True)
                group = weight_group(b - 1)
                nc.scalar.copy(w1h[:, group], w1[:, group])
                nc.scalar.copy(w2h[:, group], w2[:, group]).then_inc(split_hi, 1)
            for b in range(SPLITS + 1, NB - 1):
                attention(b, True)
            attention(NB - 1, False)
            act.wait_ge(w_ffn, ALL_FFN)
            nc.scalar.activation(aexp[:], acol[:], ACT.Exp).then_inc(aexp_ready, 1)

            def main(half, c, j):
                for half, c, j in behind(half, c, j, 0):
                    q = job(half, c)
                    act.wait_ge(hid_done, q * NH + j + 1)
                    if not isinstance(q, int) or q * NH + j >= NSB:
                        act.wait_ge(used, q * NH + j - NSB + 1)
                    nc.scalar.activation(hid[:, j % NSB], hid_ps[j % 2][:], ACT.Silu, bias=b1[:, j:j + 1]).then_inc(silu_ready, 1)

            def high_part(half, c, j):
                for half, c, j in behind(half, c, j, HI_LAG):
                    if j in SPLIT:
                        q = job(half, c)
                        n = q * NH + j
                        if not isinstance(n, int) or n >= NPB:
                            act.wait_ge(used, n - NPB + 1)
                        wait_hidden(act, q, j)
                        nc.scalar.copy(hid_hi[:, j % NPB], hid[:, j % NSB]).then_inc(hi_ready, 1)

            def step(c, t):
                act.wait_ge(u_ready, (c - 1) * TC + t + 1)
                nc.scalar.activation(st[:, :, t], u[:], ACT.Tanh).then_inc(st_ready, 1)

            def stages(half, c, j):
                for i, task in enumerate(("finish1", "finish2")):
                    if stage(half, c, j, task, "evacuate"):
                        act.wait_ge(y_done, (job(0, c) if i == 0 else job(1, c - 1)) + 1)
                        nc.scalar.activation(yT[:], y_ps[i][:], ACT.Identity, bias=sb2sum[:]).then_inc(yT_ready, 1)
                if stage(half, c, j, "prepare1", "heads"):
                    if isinstance(c, int) and c < 0:
                        act.wait_ge(heads_ready, NB)
                    else:
                        act.wait_ge(filled[1], fills(1, "prepare1", "heads", c - 1) + 1)
                    src = heads[:, :, bass.ds((c + 1) * TC, TC)]
                    nc.scalar.copy(headc[:], src).then_inc(headc_ready, 1)
                for i, task in enumerate(("prepare1", "prepare2")):
                    if stage(half, c, j, task, "transpose"):
                        act.wait_ge(filled[0], fills(0, task, "x", c) + 1)
                        nc.scalar.copy(xT[:], side[0][:]).then_inc(emptied[0], 1)
                    if stage(half, c, j, task, "tanh"):
                        act.wait_ge(route_step, job(i, c + 1 - i) * ROUTE + 3)
                        nc.scalar.activation(th[:], lg[:, 0], ACT.Tanh, scale=0.5).then_inc(gexp_ready, 1)
                if stage(half, c, j, "prepare1", "keep"):
                    if has("finish1", c):
                        act.wait_ge(emptied[0], fills(0, "finish1", "y", c) + 1)
                    nc.scalar.copy(flat(x1keep), flat(x1)).then_inc(keep1_ready, 1)
                if stage(half, c, j, "prepare2", "keep"):
                    if has("finish2", c):
                        act.wait_ge(emptied[0], fills(0, "finish2", "y", c) + 1)
                    nc.scalar.copy(flat(x3keep), flat(x3)).then_inc(keep_ready, 1)
                for i, task in enumerate(("gates1", "prepare2")):
                    if stage(half, c, j, task, "gateT"):
                        act.wait_ge(filled[0], fills(0, task, "gate", c) + 1)
                        nc.scalar.copy(gateT[i][:], side[0][:]).then_inc(emptied[0], 1)
                if stage(half, c, j, "scan_in", "transpose"):
                    act.wait_ge(filled[0], fills(0, "scan_in", "x", c) + 1)
                    nc.scalar.copy(xTs[:], side[0][:]).then_inc(emptied[0], 1)

            iterations(act, lambda c: slots(c, main, step, stages, high_part))

        @block.vector
        def _(dve):
            def ln_stats(n, x, i=0):
                for k in range(4):
                    last = nc.vector.bn_stats(stats[i][:, k], x[:, k])
                last.then_inc(ln_step[i], 1)

            def ln_aggregate(n, i=0):
                wait_apart(dve, ln_step[i], 4 * n + 1)
                for k in range(4):
                    last = nc.vector.bn_aggr(mv[i][:, k], stats[i][:, k])
                last.then_inc(ln_step[i], 1)
                dve.wait_ge(ln_step[i], 4 * n + 2)
                nc.vector.tensor_scalar(veps[i][:], mv[i][:, :, 1], EPS, None, ALU.add).then_inc(ln_step[i], 1)

            def ln_apply(n, x, y, blocks, i=0):
                dve.wait_ge(rstd_ready[i], n + 1)
                for k in blocks:
                    last = nc.vector.tensor_scalar(y[:, k], x[:, k], mv[i][:, k, 0:1], rstd[i][:, k:k + 1],
                                                   ALU.subtract, ALU.mult)
                if 3 in blocks:
                    last.then_inc(ln_step[i], 1)

            def rotate(b, i):
                dve.wait_ge(proj_done, 2 * b + i + 1)
                if not isinstance(b, int) or b > 0:
                    dve.wait_ge(qk_ready, 2 * b + i - 1)
                for h in range(2):
                    nc.vector.tensor_tensor(rot[:, 2 * i + h], proj_ps[h][:], rope[:, 2 * i + h], ALU.mult).then_inc(rot_step, 1)

            def neg_max(b, i):
                dve.wait_ge(scores_done, 4 * b + i + 1)
                nc.vector.tensor_reduce(nmax[:, i:i + 1], scores_ps[i % 2][:], AX_X, ALU.max, negate=True).then_inc(max_ready, 1)

            def row_scale(b, i):
                dve.wait_ge(exp_ready, 4 * b + i + 1)
                nc.vector.reciprocal(rinv[:, i:i + 1], rsum[:, i:i + 1]).then_inc(rinv_ready, 1)

            def decay(b, i):
                dve.wait_ge(pT_done, 4 * b + i + 1)
                if i == 0 and (not isinstance(b, int) or b > 0):
                    dve.wait_ge(av_done, b)
                decays = dtab[:, i * P:i * P + 4 * P]
                nc.vector.tensor_tensor(pd[:, :, i * P:(i + 1) * P], pT_ps[i % 2][:].rearrange("p (k q) -> p k q", k=4),
                                        decays.rearrange("p (k q) -> p k q", k=4), ALU.mult).then_inc(pd_ready, 1)

            def ln_begin(b):
                dve.wait_ge(x_in, 16 * (b + 1))
                ln_stats(b, xin)
                ln_aggregate(b)

            def ln_end(b):
                if not isinstance(b, int) or b > 0:
                    dve.wait_ge(xT_ready, b)
                ln_apply(b, xin, xn, range(4))

            def attention(b, more, still_more):
                neg_max(b, 0)
                neg_max(b, 1)
                row_scale(b, 0)
                row_scale(b, 1)
                if more:
                    rotate(b + 1, 0)
                neg_max(b, 2)
                neg_max(b, 3)
                row_scale(b, 2)
                decay(b, 0)
                row_scale(b, 3)
                decay(b, 1)
                decay(b, 2)
                decay(b, 3)
                if still_more:
                    ln_begin(b + 2)
                if more:
                    rotate(b + 1, 1)
                if still_more:
                    ln_end(b + 2)

            ln_begin(0)
            ln_end(0)
            dve.wait_ge(w_rope, 16)
            rotate(0, 0)
            rotate(0, 1)
            ln_begin(1)
            ln_end(1)
            dve.wait_ge(w_decay, 16)
            attention(0, True, True)
            with dve.Fori(1, NB - 2) as b:
                attention(b, True, True)
            attention(NB - 2, True, False)
            attention(NB - 1, False, False)
            dve.wait_ge(split_b, 1)
            nc.vector.tensor_tensor(b2l[:], b2raw[:], b2h[:].bitcast(F32), ALU.subtract)
            nc.vector.tensor_tensor(sb2sum[:], sb2[:, 0:1], sb2[:, 1:2], ALU.add).then_inc(split_done, 1)
            dve.wait_ge(aexp_ready, 1)

            def main(half, c, j):
                for half, c, j in behind(half, c, j, GATE_LAG):
                    if j >= NS:
                        q = job(half, c)
                        dve.wait_ge(silu_ready, q * NH + j + 1)
                        dve.wait_ge(gateb_done, q * NR + j - NS + 1)
                        nc.vector.tensor_tensor(hid[:, j % NSB], gate_ps[j % 2][:], hid[:, j % NSB], ALU.mult).then_inc(gated_ready, 1)

            def low_part(half, c, j):
                for half, c, j in behind(half, c, j, LO_LAG):
                    if j in LO_DVE:
                        dve.wait_ge(hi_ready, nth(SPLIT, job(half, c), j))
                        nc.vector.tensor_tensor(hid_lo[:, j % NPB], hid[:, j % NSB], hid_hi[:, j % NPB].bitcast(F32),
                                                ALU.subtract).then_inc(lo_dve, 1)

            def step(c, t):
                s = (c - 1) * TC + t
                if t == 0:
                    dve.wait_ge(emptied[1], fills(1, "scan_in", "bu", c - 1) + 1)
                if not isinstance(s, int) or s > 0:
                    dve.wait_ge(st_ready, s)
                nc.vector.scalar_tensor_tensor(u[:], st[:, :, (t - 1) % TC], aexp[:], bu[:, :, t],
                                               ALU.mult, ALU.add).then_inc(u_ready, 1)

            def spread(cols, n):
                return cols.broadcast_to([P, G, n])

            def stages(half, c, j):
                for i, task in enumerate(("finish1", "finish2")):
                    if stage(half, c, j, task, "add"):
                        dve.wait_ge(filled[0], fills(0, task, "y", c) + 1)
                        if i == 0:
                            dve.wait_ge(keep1_ready, c + 1)
                            nc.vector.tensor_tensor(flat(x2), side[0][:], flat(x1keep), ALU.add).then_inc(emptied[0], 1)
                        else:
                            if not isinstance(c, int) or c > 3:
                                dve.wait_ge(stored, 32 * (c - 3))
                            dve.wait_ge(keep_ready, c - 2)
                            nc.vector.tensor_tensor(flat(fin), side[0][:], flat(x3keep), ALU.add).then_inc(emptied[0], 1)
                for i, task in enumerate(("prepare1", "prepare2")):
                    x = (x1, x3)[i]
                    if i == 0 and stage(half, c, j, task, "x"):
                        dve.wait_ge(filled[1], fills(1, task, "heads", c) + 1)
                        dve.wait_ge(xres_in, 32 * (c + 2))
                        if not isinstance(c, int) or c >= 0:
                            dve.wait_ge(keep1_ready, c + 1)
                        nc.vector.tensor_tensor(flat(x1), side[1][:], flat(xres), ALU.add).then_inc(emptied[1], 1)
                    if stage(half, c, j, task, "stats"):
                        if i == 0:
                            dve.wait_ge(emptied[1], fills(1, task, "heads", c) + 1)
                        else:
                            dve.wait_ge(emptied[1], fills(1, "scan_out", "y", c - 1) + 1)
                        ln_stats(norms(task, c), x)
                    if stage(half, c, j, task, "aggregate"):
                        ln_aggregate(norms(task, c))
                    for k in (0, 2):
                        if stage(half, c, j, task, f"apply{k}"):
                            ln_apply(norms(task, c), x, xn, (k, k + 1))
                    q = job(i, c + 1 - i)
                    r = q * ROUTE
                    if stage(half, c, j, task, "low"):
                        dve.wait_ge(xh_ready, q + 1)
                        nc.vector.tensor_tensor(xl[i][:], xT[:], xh[i][:].bitcast(F32), ALU.subtract).then_inc(xl_ready, 1)
                    if stage(half, c, j, task, "maxima"):
                        before_logits = fills(1, task, "logits", c)
                        dve.wait_ge(filled[1], before_logits + 1)
                        nc.vector.tensor_tensor(lg[:, 0], side[1][:, 0:G * NE].rearrange("p (k e) -> p k e", k=G),
                                                rb[:].rearrange("p (o e) -> p o e", o=1).broadcast_to([P, G, NE]),
                                                ALU.add).then_inc(emptied[1], 1)
                        wait_apart(dve, emptied[1], before_logits + 1)
                        for k in range(G):
                            last = nc.vector.max(top[:, k], lg[:, 0, k])
                        last.then_inc(route_step, 1)
                    if stage(half, c, j, task, "replace"):
                        wait_apart(dve, route_step, r + 1)
                        for k in range(G):
                            last = nc.vector.match_replace(lg[:, 1, k], top[:, k], lg[:, 0, k], LOWEST)
                        last.then_inc(route_step, 1)
                    if stage(half, c, j, task, "below_max"):
                        dve.wait_ge(route_step, r + 2)
                        nc.vector.tensor_tensor(lg[:, 0], lg[:, 0], spread(top[:, :, 0:1], NE), ALU.subtract).then_inc(route_step, 1)
                    if stage(half, c, j, task, "reciprocal"):
                        dve.wait_ge(gexp_ready, q + 1)
                        nc.vector.tensor_scalar(den[:], th[:], -1.0, 1.0, ALU.mult, ALU.add).then_inc(route_step, 1)
                        dve.wait_ge(route_step, r + 4)
                        nc.vector.reciprocal(den[:], den[:]).then_inc(route_step, 1)
                    if stage(half, c, j, task, "choose"):
                        dve.wait_ge(route_step, r + 5)
                        nc.vector.scalar_tensor_tensor(gate[:], th[:], 1.0, den[:], ALU.add, ALU.mult).then_inc(route_step, 1)
                        dve.wait_ge(route_step, r + 6)
                        nc.vector.scalar_tensor_tensor(gate[:], lg[:, 1], LOWEST, gate[:], ALU.is_le, ALU.mult).then_inc(route_step, 1)
                    if stage(half, c, j, task, "scale"):
                        dve.wait_ge(route_step, r + 7)
                        nc.vector.tensor_reduce(gsum[:], gate[:], AX_X, ALU.add).then_inc(route_step, 1)
                        dve.wait_ge(route_step, r + 8)
                        nc.vector.reciprocal(ginv[:], gsum[:]).then_inc(route_step, 1)
                        dve.wait_ge(route_step, r + 9)
                        nc.vector.tensor_tensor(gate[:], gate[:], spread(ginv[:].rearrange("p (k o) -> p k o", o=1), NE), ALU.mult).then_inc(route_step, 1)
                    if stage(half, c, j, task, "split"):
                        dve.wait_ge(route_step, r + 10)
                        nc.vector.tensor_copy(gate2[:, :, 0].bitcast(F32R), gate[:]).then_inc(route_step, 1)
                        dve.wait_ge(route_step, r + 11)
                        nc.vector.tensor_tensor(gate2[:, :, 1].bitcast(F32R), gate[:], gate2[:, :, 0], ALU.subtract).then_inc(route_step, 1)
                if stage(half, c, j, "scan_out", "add"):
                    dve.wait_ge(filled[1], fills(1, "scan_out", "y", c) + 1)
                    if not isinstance(c, int) or c >= 2:
                        dve.wait_ge(keep_ready, c - 1)
                    nc.vector.tensor_tensor(flat(x3), side[1][:], flat(x2d), ALU.add).then_inc(emptied[1], 1)
                if stage(half, c, j, "scan_in", "stats"):
                    dve.wait_ge(emptied[0], fills(0, "finish1", "y", c) + 1)
                    ln_stats(norms("scan_in", c), x2, 1)
                if stage(half, c, j, "scan_in", "aggregate"):
                    ln_aggregate(norms("scan_in", c), 1)
                for k in (0, 2):
                    if stage(half, c, j, "scan_in", f"apply{k}"):
                        ln_apply(norms("scan_in", c), x2, xns, (k, k + 1), 1)
                if stage(half, c, j, "scan_in", "bu"):
                    dve.wait_ge(filled[1], fills(1, "scan_in", "bu", c) + 1)
                    nc.vector.tensor_scalar(bu[:].rearrange("p g t -> p (g t)"), side[1][:, 0:2 * TC], bb[:], None,
                                            ALU.add).then_inc(emptied[1], 1)
                if stage(half, c, j, "scan_in", "add"):
                    dve.wait_ge(filled[1], fills(1, "scan_in", "direct", c) + 1)
                    nc.vector.tensor_tensor(flat(x2d), side[1][:], flat(x2), ALU.add).then_inc(emptied[1], 1)

            iterations(dve, lambda c: slots(c, main, step, stages, low_part))

        @block.tensor
        def _(pe):
            def transpose4(dst, parts):
                for k in range(4):
                    last = nc.tensor.transpose(dst[:, k * P:(k + 1) * P], parts(k), idn[:])
                return last

            def transposed_x(b):
                pe.wait_ge(ln_step[0], 4 * b + 4)
                if not isinstance(b, int) or b > 0:
                    pe.wait_ge(rot_step, 4 * b)
                transpose4(proj_ps[1], lambda k: xn[:, k]).then_inc(lnT_ps, 1)

            def project(b, i):
                if i == 0:
                    pe.wait_ge(xT_ready, b + 1)
                if not isinstance(b, int) or b > 0 or i > 0:
                    pe.wait_ge(rot_step, 4 * b + 2 * i)
                for h in range(2):
                    last = nc.tensor.matmul(proj_ps[h][:], wqk[:, 2 * i + h], xT[:], start=True, stop=True)
                last.then_inc(proj_done, 1)

            def values(b):
                pe.wait_ge(xT_ready, b + 1)
                if not isinstance(b, int) or b > 0:
                    pe.wait_ge(v_ready, b)
                for k in range(4):
                    last = nc.tensor.matmul(side_ps[:, k * P:(k + 1) * P], xT[:, k * P:(k + 1) * P], wv[:],
                                            start=True, stop=True)
                last.then_inc(v_ps, 1)

            def score(b, i):
                if i == 0:
                    pe.wait_ge(qk_ready, 2 * b + 2)
                if i >= 2:
                    pe.wait_ge(exp_ready, 4 * b + i - 1)
                nc.tensor.matmul(scores_ps[i % 2][:], qT[:, i * P:(i + 1) * P], kT[:], start=True, stop=True).then_inc(scores_done, 1)

            def weights(b, i):
                pe.wait_ge(norm_ready, 4 * b + i + 1)
                if i >= 2:
                    pe.wait_ge(pd_ready, 4 * b + i - 1)
                transpose4(pT_ps[i % 2], lambda k: p[:, i, (3 - k) * P:(4 - k) * P]).then_inc(pT_done, 1)

            def attend(b):
                pe.wait_ge(pd_ready, 4 * b + 4)
                pe.wait_ge(v_ready, b + 1)
                if not isinstance(b, int) or b > 0:
                    pe.wait_ge(heads_ready, b)
                for k in range(4):
                    last = nc.tensor.matmul(heads_ps[:], v[:, 3 - k], pd[:, k], start=(k == 0), stop=(k == 3))
                last.then_inc(av_done, 1)

            def attention(b, more):
                score(b, 0)
                if more:
                    transposed_x(b + 1)
                score(b, 1)
                if more:
                    project(b + 1, 0)
                score(b, 2)
                score(b, 3)
                weights(b, 0)
                weights(b, 1)
                if more:
                    project(b + 1, 1)
                weights(b, 2)
                weights(b, 3)
                if more:
                    values(b + 1)
                attend(b)

            pe.wait_ge(w_ident, 16)
            transposed_x(0)
            pe.wait_ge(w_proj, 32)
            project(0, 0)
            project(0, 1)
            values(0)
            attention(0, True)
            with pe.Fori(1, NB - 1) as b:
                attention(b, True)
            attention(NB - 1, False)
            pe.wait_ge(split_done, 1)
            pe.wait_ge(sel_ready, 1)
            pe.wait_ge(split_lo, SPLITS)
            pe.wait_ge(consts_ready, 1)

            def second_product(half, c, j):
                q = job(half, c)
                cols = slice(j * D, (j + 1) * D)
                if j in SPLIT:
                    high, low = hid_hi[:, j % NPB], hid_lo[:, j % NPB]
                    pe.wait_ge(hi_ready, nth(SPLIT, q, j))
                    nc.tensor.matmul(y_ps[half][:], w2l[:, cols], high, start=(j == 0), stop=False)
                    nc.tensor.matmul(y_ps[half][:], w2h[:, cols], high, start=False, stop=False)
                    if j in LO_POOL:
                        pe.wait_ge(lo_pool, nth(LO_POOL, q, j))
                    else:
                        pe.wait_ge(lo_dve, nth(LO_DVE, q, j))
                    nc.tensor.matmul(y_ps[half][:], w2h[:, cols], low, start=False, stop=False).then_inc(used, 1)
                else:
                    wait_hidden(pe, q, j)
                    nc.tensor.matmul(y_ps[half][:], w2[:, cols], hid[:, j % NSB], start=False, stop=False).then_inc(used, 1)
                if j == NH - 1:
                    nc.tensor.matmul(y_ps[half][:], b2l[:], gateT[half][:], start=False, stop=False)
                    nc.tensor.matmul(y_ps[half][:], b2h[:], gateT[half][:], start=False, stop=True).then_inc(y_done, 1)

            def first_product(half, c, j):
                q = job(half, c)
                n = q * NH + j
                r = q * NR + j - NS
                if j == 0:
                    pe.wait_ge(xl_ready, q + 1)
                if not isinstance(n, int) or n >= 2:
                    pe.wait_ge(silu_ready, n - 1)
                cols = slice(j * P, (j + 1) * P)
                nc.tensor.matmul(hid_ps[j % 2][:], w1l[:, cols], xh[half][:], start=True, stop=False)
                nc.tensor.matmul(hid_ps[j % 2][:], w1h[:, cols], xl[half][:], start=False, stop=False)
                nc.tensor.matmul(hid_ps[j % 2][:], w1h[:, cols], xh[half][:], start=False, stop=True).then_inc(hid_done, 1)
                if j >= NS:
                    if j == NS:
                        task = ("gates1", "prepare2")[half]
                        pe.wait_ge(emptied[0], fills(0, task, "gate", c) + 1)
                    if not isinstance(r, int) or r >= 2:
                        pe.wait_ge(gated_ready, r - 1)
                    g = j - NS
                    nc.tensor.matmul(gate_ps[j % 2][:], sel[:, g * P:(g + 1) * P], gateT[half][:],
                                     start=True, stop=True).then_inc(gateb_done, 1)

            def main(half, c, j):
                for chunk in behind(half, c, j, 0):
                    first_product(*chunk)
                for chunk in behind(half, c, j, LAG):
                    second_product(*chunk)

            def fill(bank, task, what, c):
                n = fills(bank, task, what, c)
                if not isinstance(n, int) or n > 0:
                    pe.wait_ge(emptied[bank], n)

            def stages(half, c, j):
                for i, task in enumerate(("finish1", "finish2")):
                    if stage(half, c, j, task, "transpose"):
                        pe.wait_ge(yT_ready, (job(0, c) if i == 0 else job(1, c - 1)) + 1)
                        fill(0, task, "y", c)
                        transpose4(side[0], lambda k: yT[:, k * P:(k + 1) * P]).then_inc(filled[0], 1)
                if stage(half, c, j, "prepare1", "heads_transpose"):
                    pe.wait_ge(headc_ready, c + 2)
                    fill(1, "prepare1", "heads", c)
                    transpose4(side[1], lambda k: headc[:, 2 * k:2 * k + 2].rearrange("p g t -> p (g t)")).then_inc(filled[1], 1)
                for i, task in enumerate(("prepare1", "prepare2")):
                    if stage(half, c, j, task, "transpose"):
                        pe.wait_ge(ln_step[0], 4 * norms(task, c) + 4)
                        fill(0, task, "x", c)
                        transpose4(side[0], lambda k: xn[:, k]).then_inc(filled[0], 1)
                    if stage(half, c, j, task, "logits"):
                        pe.wait_ge(emptied[0], fills(0, task, "x", c) + 1)
                        fill(1, task, "logits", c)
                        for k in range(G):
                            last = nc.tensor.matmul(side[1][:, k * NE:(k + 1) * NE], xT[:, k * P:(k + 1) * P], rw[:],
                                                    start=True, stop=True)
                        last.then_inc(filled[1], 1)
                for i, task in enumerate(("gates1", "prepare2")):
                    if stage(half, c, j, task, "gateT"):
                        pe.wait_ge(route_step, (job(i, c) + 1) * ROUTE)
                        fill(0, task, "gate", c)
                        transpose4(side[0], lambda k: gate2[:, k].rearrange("p h e -> p (h e)")).then_inc(filled[0], 1)
                if stage(half, c, j, "scan_out", "product"):
                    pe.wait_ge(st_ready, c * TC)
                    fill(1, "scan_out", "y", c)
                    for k in range(G):
                        last = nc.tensor.matmul(side[1][:, k * P:(k + 1) * P], st[:].rearrange("p g t -> p (g t)"),
                                                ck[:, k], start=True, stop=True)
                    last.then_inc(filled[1], 1)
                if stage(half, c, j, "scan_in", "transpose"):
                    pe.wait_ge(ln_step[1], 4 * norms("scan_in", c) + 4)
                    fill(0, "scan_in", "x", c)
                    transpose4(side[0], lambda k: xns[:, k]).then_inc(filled[0], 1)
                if stage(half, c, j, "scan_in", "bu"):
                    pe.wait_ge(emptied[0], fills(0, "scan_in", "x", c) + 1)
                    fill(1, "scan_in", "bu", c)
                    for k in range(G):
                        last = nc.tensor.matmul(side[1][k * STATE:(k + 1) * STATE, 0:P], bwT[:], xTs[:, k * P:(k + 1) * P],
                                                start=True, stop=True)
                    last.then_inc(filled[1], 1)
                if stage(half, c, j, "scan_in", "direct"):
                    fill(1, "scan_in", "direct", c)
                    for k in range(G):
                        dst = side[1][:, k * P:(k + 1) * P]
                        nc.tensor.matmul(dst, xTs[:, k * P:(k + 1) * P], dwT[:], start=True, stop=False)
                        last = nc.tensor.matmul(dst, ones2[:], cd[:], start=False, stop=True)
                    last.then_inc(filled[1], 1)

            iterations(pe, lambda c: slots(c, main, None, stages))


def tables():
    half = D // 2
    f = np.float32
    scale_vec = (np.arange(0, D, 2, dtype=f) + f(0.4 * D)) / f(1.4 * D)
    power = np.arange(L, dtype=f) / f(SCALE_BASE)
    scale = (scale_vec[None, :] ** power[:, None]).astype(f)
    inv_freq = (f(1.0) / f(10000.0) ** (np.arange(half, dtype=f) / f(half))).astype(f)
    angle = np.arange(L, dtype=f)[:, None] * inv_freq[None, :]
    sign = np.where(np.arange(D) % 2 == 0, f(-1), f(1))[None, :]
    rows = []
    for s in (scale, f(1.0) / scale):
        rows.append(np.repeat(np.cos(angle) * s, 2, axis=-1).T)
        rows.append((np.repeat(np.sin(angle) * s, 2, axis=-1) * sign).T)
    ropes = np.ascontiguousarray(np.stack(rows, axis=1), dtype=f)
    i = np.arange(3 * P + L)[None, :]
    decay = (GAMMA ** np.abs(i - 3 * P - np.arange(P)[:, None])).astype(f)
    sel = np.zeros((P, NR, P), f)
    for j in range(NR):
        for m in range(P):
            e = j * (P // HE) + m // HE
            sel[e, j, m] = sel[NE + e, j, m] = 1.0
    return ropes, decay, np.eye(P, dtype=f), sel.reshape(P, NR * P)


def kernel(**inputs):
    import concourse.bacc as bacc
    from concourse.bass_utils import run_bass_kernel_spmd

    a = {k.replace("L0_", ""): np.asarray(v) for k, v in inputs.items()}
    swap = np.arange(D) ^ 1
    wq, wk = a["attn_a_W_Q"], a["attn_a_W_K"]
    ropes, decay, eye, sel = tables()
    ck = np.zeros((P, G, D), np.float32)
    for k in range(G):
        ck[k * STATE:(k + 1) * STATE, k] = a["attn_b_C_w"].T
    w1 = np.concatenate([a["ffn_sw1"].transpose(1, 0, 2).reshape(D, NS * P),
                         a["ffn_w1"].transpose(1, 0, 2).reshape(D, NR * P)], axis=1)
    w2 = np.concatenate([a["ffn_sw2"].reshape(NS, P, D), a["ffn_w2"].reshape(NR, P, D)]).transpose(1, 0, 2)
    b1 = np.concatenate([a["ffn_sb1"].reshape(NS, P), a["ffn_b1"].reshape(NR, P)]).T
    arrays = {
        "X": a["attn_a_X"],
        "Wqk": np.stack([wq, wq[:, swap], wk, wk[:, swap]], axis=1),
        "Wv": a["attn_a_W_V"], "ropes": ropes, "Dtab": decay, "ident": eye,
        "W1": w1, "W2": w2.reshape(P, NH * D), "B1": b1, "B2": np.concatenate([a["ffn_b2"]] * 2), "SB2": a["ffn_sb2"].T,
        "RW": a["ffn_router_w"], "RB": np.tile(a["ffn_router_b"][None], (P, 1)), "Sel": sel,
        "Acol": np.tile(a["attn_b_A"], G)[:, None], "BwT": a["attn_b_B_w"].T,
        "Bb": np.tile(a["attn_b_B_b"], G)[:, None], "Ck": ck,
        "CD": np.stack([a["attn_b_C_b"], a["attn_b_D_b"]]), "DwT": a["attn_b_D_w"].T,
    }
    arrays = {k: np.ascontiguousarray(x) for k, x in arrays.items()}
    nc = bacc.Bacc("TRN2", target_bir_lowering=False, num_devices=1)
    aps = [nc.dram_tensor(k, x.shape, F32, kind="ExternalInput").ap() for k, x in arrays.items()]
    out = nc.dram_tensor("out", (NB, L, D), F32, kind="ExternalOutput").ap()
    program(nc, *aps, out)
    r = run_bass_kernel_spmd(nc, [arrays], core_ids=[0])
    return r.results[0]["out"]
```
